# Optimizing a Trainium2 kernel written in Bass

```python
import numpy as np
import jax
import jax.numpy as jnp

def _softmax(x, axis=-1):
    return jax.nn.softmax(x, axis=axis)

def _gelu(x):
    return jax.nn.gelu(x, approximate=True)

def _silu(x):
    return jax.nn.silu(x)

def _sigmoid(x):
    return jax.nn.sigmoid(x)

def _layernorm(x, axis=-1, eps=1e-05):
    m = jnp.mean(x, axis=axis, keepdims=True)
    v = jnp.var(x, axis=axis, keepdims=True)
    return (x - m) / jnp.sqrt(v + eps)

def _scatter_add(tgt, idx, src, axis=0):
    return tgt.at[idx].add(src)

def _segment_sum(src, seg, n):
    return jax.ops.segment_sum(src, seg, n)
kernel_name = 'mk_conv_attn_hybrid_d4_conv_nchw512_r4_a5e32b'

def setup_inputs(seed: int=0):
    np.random.seed(seed)
    _w = jnp.asarray

    def _rec_inputs():
        import jax
        import jax.numpy as jnp
        _gk = jax.random.key(seed)
        x = 7.22e-05 + 1 * jax.random.normal(jax.random.fold_in(_gk, 1), (4, 128, 16, 16), jnp.float32)
        return x
    x = _rec_inputs()

    def _L0_conv_setup():
        import jax, jax.numpy as jnp
        import numpy as np
        NUM_GROUPS = 32
        EPS = 1e-06

        def group_norm(x, gamma, beta):
            B, C, H, W = x.shape
            xg = x.reshape(B, NUM_GROUPS, C // NUM_GROUPS, H, W)
            mean = xg.mean(axis=(2, 3, 4), keepdims=True)
            var = xg.var(axis=(2, 3, 4), keepdims=True)
            xn = ((xg - mean) * jax.lax.rsqrt(var + EPS)).reshape(B, C, H, W)
            return xn * gamma[None, :, None, None] + beta[None, :, None, None]

        def conv1x1(x, w, b):
            return jnp.einsum('oc,bchw->bohw', w, x) + b[None, :, None, None]
        key = jax.random.key(seed)
        ks = jax.random.split(key, 12)
        B, C, H, W = (4, 128, 16, 16)
        s = 1.0 / np.sqrt(C)
        inp = {'x': jax.random.normal(ks[0], (B, C, H, W), dtype=jnp.float32), 'norm_gamma': jnp.ones((C,), jnp.float32), 'norm_beta': jnp.zeros((C,), jnp.float32), 'wq': jax.random.normal(ks[1], (C, C), jnp.float32) * s, 'bq': jnp.zeros((C,), jnp.float32), 'wk': jax.random.normal(ks[2], (C, C), jnp.float32) * s, 'bk': jnp.zeros((C,), jnp.float32), 'wv': jax.random.normal(ks[3], (C, C), jnp.float32) * s, 'bv': jnp.zeros((C,), jnp.float32), 'wp': jax.random.normal(ks[4], (C, C), jnp.float32) * s, 'bp': jnp.zeros((C,), jnp.float32)}
        return inp
    _L0_conv_all = _L0_conv_setup()
    _L0_conv_in = {k: v for k, v in _L0_conv_all.items() if k in ('norm_gamma', 'norm_beta', 'wq', 'bq', 'wk', 'bk', 'wv', 'bv', 'wp', 'bp')}
    del _L0_conv_all

    def _L1_conv_setup():
        import jax, jax.numpy as jnp
        import numpy as np
        key = jax.random.key(seed)
        ks = jax.random.split(key, 7)
        N, C_in, H, W = (32, 128, 56, 56)
        C_sq, C_e1, C_e3 = (16, 64, 64)
        return {'x': jax.random.normal(ks[0], (N, C_in, H, W), dtype=jnp.float32), 'squeeze_w': jax.random.normal(ks[1], (C_sq, C_in), dtype=jnp.float32) * 0.05, 'squeeze_b': jax.random.normal(ks[2], (C_sq,), dtype=jnp.float32) * 0.05, 'expand1x1_w': jax.random.normal(ks[3], (C_e1, C_sq), dtype=jnp.float32) * 0.05, 'expand1x1_b': jax.random.normal(ks[4], (C_e1,), dtype=jnp.float32) * 0.05, 'expand3x3_w': jax.random.normal(ks[5], (C_e3, C_sq, 3, 3), dtype=jnp.float32) * 0.05, 'expand3x3_b': jax.random.normal(ks[6], (C_e3,), dtype=jnp.float32) * 0.05}
    _L1_conv_all = _L1_conv_setup()
    _L1_conv_in = {k: v for k, v in _L1_conv_all.items() if k in ('squeeze_w', 'squeeze_b', 'expand1x1_w', 'expand1x1_b', 'expand3x3_w', 'expand3x3_b')}
    del _L1_conv_all

    def _L2_attn_setup():
        import jax, jax.numpy as jnp
        import numpy as np
        NHEAD = 8
        WINDOW = 64

        def _sliding_window_attention(q, k, v, w):
            B, H, S, D = q.shape
            assert S % w == 0
            nb = S // w
            qb = q.reshape(B, H, nb, w, D)
            kb = k.reshape(B, H, nb, w, D)
            vb = v.reshape(B, H, nb, w, D)
            k_prev = jnp.pad(kb, ((0, 0), (0, 0), (1, 0), (0, 0), (0, 0)))[:, :, :nb]
            v_prev = jnp.pad(vb, ((0, 0), (0, 0), (1, 0), (0, 0), (0, 0)))[:, :, :nb]
            k2 = jnp.concatenate([k_prev, kb], axis=3)
            v2 = jnp.concatenate([v_prev, vb], axis=3)
            scores = jnp.einsum('bhnqd,bhnkd->bhnqk', qb, k2) / jnp.sqrt(jnp.asarray(D, q.dtype))
            qi = jnp.arange(w)[:, None]
            ki = jnp.arange(2 * w)[None, :]
            valid = (ki >= qi + 1) & (ki <= qi + w)
            n_idx = jnp.arange(nb)[:, None, None]
            valid = valid[None] & ((n_idx > 0) | (ki[None] >= w))
            neg = jnp.asarray(-1e+30, scores.dtype)
            scores = jnp.where(valid[None, None], scores, neg)
            attn = jax.nn.softmax(scores, axis=-1)
            out = jnp.einsum('bhnqk,bhnkd->bhnqd', attn, v2)
            return out.reshape(B, H, S, D)
        key = jax.random.key(seed)
        ks = jax.random.split(key, 5)
        B, S, Dm = (2, 2048, 128)
        x = jax.random.normal(ks[0], (B, S, Dm), jnp.float32)
        w_scale = 0.02
        Wq = jax.random.normal(ks[1], (Dm, Dm), jnp.float32) * w_scale
        Wk = jax.random.normal(ks[2], (Dm, Dm), jnp.float32) * w_scale
        Wv = jax.random.normal(ks[3], (Dm, Dm), jnp.float32) * w_scale
        Wo = jax.random.normal(ks[4], (Dm, Dm), jnp.float32) * w_scale
        return {'x': x, 'Wq': Wq, 'Wk': Wk, 'Wv': Wv, 'Wo': Wo}
    _L2_attn_all = _L2_attn_setup()
    _L2_attn_in = {k: v for k, v in _L2_attn_all.items() if k in ('Wq', 'Wk', 'Wv', 'Wo')}
    del _L2_attn_all

    def _L2_ffn_setup():
        import jax, jax.numpy as jnp
        import numpy as np
        IN_FEATURES = 128
        FEATURES = 128
        BATCH, SEQ = (8, 2048)

        def _ste(x_orig, y_proc):
            return x_orig + jax.lax.stop_gradient(y_proc - x_orig)
        key = jax.random.key(seed)
        kx, kw = jax.random.split(key)
        x = jax.random.normal(kx, (BATCH, SEQ, IN_FEATURES), dtype=jnp.float32)
        weight = jax.random.normal(kw, (IN_FEATURES, FEATURES), dtype=jnp.float32) / np.sqrt(IN_FEATURES)
        bias = jnp.zeros((FEATURES,), dtype=jnp.float32)
        return {'x': x, 'weight': weight, 'bias': bias}
    _L2_ffn_all = _L2_ffn_setup()
    _L2_ffn_in = {k: v for k, v in _L2_ffn_all.items() if k in ('weight', 'bias')}
    del _L2_ffn_all

    def _L3_attn_setup():
        import jax, jax.numpy as jnp
        import numpy as np
        D_HEAD = 16
        key = jax.random.key(seed)
        k1, k2, k3, k4, k5 = jax.random.split(key, 5)
        b, s, d_model, n_heads, d_head = (2, 1024, 128, 8, D_HEAD)
        x = jax.random.normal(k1, (b, s, d_model), dtype=jnp.float32)
        scale = 1.0 / np.sqrt(d_model)
        W_K = jax.random.normal(k2, (n_heads, d_head, d_model), dtype=jnp.float32) * scale
        W_Q = jax.random.normal(k3, (n_heads, d_head, d_model), dtype=jnp.float32) * scale
        W_V = jax.random.normal(k4, (n_heads, d_head, d_model), dtype=jnp.float32) * scale
        W_O = jax.random.normal(k5, (d_model, d_head * n_heads), dtype=jnp.float32) * scale
        return {'x': x, 'W_K': W_K, 'W_Q': W_Q, 'W_V': W_V, 'W_O': W_O}
    _L3_attn_all = _L3_attn_setup()
    _L3_attn_in = {k: v for k, v in _L3_attn_all.items() if k in ('W_K', 'W_Q', 'W_V', 'W_O')}
    del _L3_attn_all

    def _L3_ffn_setup():
        import jax, jax.numpy as jnp
        import numpy as np
        TOP_K = 2
        key = jax.random.key(seed)
        ks = jax.random.split(key, 6)
        B, T, C, E, H = (4, 1024, 128, 8, 512)
        x = jax.random.normal(ks[0], (B, T, C), dtype=jnp.float32)
        W_router = jax.random.normal(ks[1], (C, E), dtype=jnp.float32) * 0.02
        W1 = jax.random.normal(ks[2], (E, C, H), dtype=jnp.float32) * 0.02
        b1 = jnp.zeros((E, H), dtype=jnp.float32)
        W2 = jax.random.normal(ks[3], (E, H, C), dtype=jnp.float32) * 0.02
        b2 = jnp.zeros((E, C), dtype=jnp.float32)
        return {'x': x, 'W_router': W_router, 'W1': W1, 'b1': b1, 'W2': W2, 'b2': b2}
    _L3_ffn_all = _L3_ffn_setup()
    _L3_ffn_in = {k: v for k, v in _L3_ffn_all.items() if k in ('W_router', 'W1', 'b1', 'W2', 'b2')}
    del _L3_ffn_all
    return {'x': x, 'L0_conv_norm_gamma': _L0_conv_in['norm_gamma'], 'L0_conv_norm_beta': _L0_conv_in['norm_beta'], 'L0_conv_wq': _L0_conv_in['wq'], 'L0_conv_bq': _L0_conv_in['bq'], 'L0_conv_wk': _L0_conv_in['wk'], 'L0_conv_bk': _L0_conv_in['bk'], 'L0_conv_wv': _L0_conv_in['wv'], 'L0_conv_bv': _L0_conv_in['bv'], 'L0_conv_wp': _L0_conv_in['wp'], 'L0_conv_bp': _L0_conv_in['bp'], 'L1_conv_squeeze_w': _L1_conv_in['squeeze_w'], 'L1_conv_squeeze_b': _L1_conv_in['squeeze_b'], 'L1_conv_expand1x1_w': _L1_conv_in['expand1x1_w'], 'L1_conv_expand1x1_b': _L1_conv_in['expand1x1_b'], 'L1_conv_expand3x3_w': _L1_conv_in['expand3x3_w'], 'L1_conv_expand3x3_b': _L1_conv_in['expand3x3_b'], 'L2_attn_Wq': _L2_attn_in['Wq'], 'L2_attn_Wk': _L2_attn_in['Wk'], 'L2_attn_Wv': _L2_attn_in['Wv'], 'L2_attn_Wo': _L2_attn_in['Wo'], 'L2_ffn_weight': _L2_ffn_in['weight'], 'L2_ffn_bias': _L2_ffn_in['bias'], 'L3_attn_W_K': _L3_attn_in['W_K'], 'L3_attn_W_Q': _L3_attn_in['W_Q'], 'L3_attn_W_V': _L3_attn_in['W_V'], 'L3_attn_W_O': _L3_attn_in['W_O'], 'L3_ffn_W_router': _L3_ffn_in['W_router'], 'L3_ffn_W1': _L3_ffn_in['W1'], 'L3_ffn_b1': _L3_ffn_in['b1'], 'L3_ffn_W2': _L3_ffn_in['W2'], 'L3_ffn_b2': _L3_ffn_in['b2']}

def reference(x, L0_conv_norm_gamma, L0_conv_norm_beta, L0_conv_wq, L0_conv_bq, L0_conv_wk, L0_conv_bk, L0_conv_wv, L0_conv_bv, L0_conv_wp, L0_conv_bp, L1_conv_squeeze_w, L1_conv_squeeze_b, L1_conv_expand1x1_w, L1_conv_expand1x1_b, L1_conv_expand3x3_w, L1_conv_expand3x3_b, L2_attn_Wq, L2_attn_Wk, L2_attn_Wv, L2_attn_Wo, L2_ffn_weight, L2_ffn_bias, L3_attn_W_K, L3_attn_W_Q, L3_attn_W_V, L3_attn_W_O, L3_ffn_W_router, L3_ffn_W1, L3_ffn_b1, L3_ffn_W2, L3_ffn_b2):
    import jax
    import jax.numpy as jnp

    def _L0_conv_ref(x, norm_gamma, norm_beta, wq, bq, wk, bk, wv, bv, wp, bp):
        import jax, jax.numpy as jnp
        import numpy as np
        NUM_GROUPS = 32
        EPS = 1e-06

        def group_norm(x, gamma, beta):
            B, C, H, W = x.shape
            xg = x.reshape(B, NUM_GROUPS, C // NUM_GROUPS, H, W)
            mean = xg.mean(axis=(2, 3, 4), keepdims=True)
            var = xg.var(axis=(2, 3, 4), keepdims=True)
            xn = ((xg - mean) * jax.lax.rsqrt(var + EPS)).reshape(B, C, H, W)
            return xn * gamma[None, :, None, None] + beta[None, :, None, None]

        def conv1x1(x, w, b):
            return jnp.einsum('oc,bchw->bohw', w, x) + b[None, :, None, None]
        B, C, H, W = x.shape
        N = H * W
        h = group_norm(x, norm_gamma, norm_beta)
        q = conv1x1(h, wq, bq).reshape(B, C, N)
        k = conv1x1(h, wk, bk).reshape(B, C, N)
        v = conv1x1(h, wv, bv).reshape(B, C, N)
        scale = jnp.asarray(C, x.dtype) ** (-0.5)
        scores = jnp.einsum('bci,bcj->bij', q, k) * scale
        w = jax.nn.softmax(scores, axis=2)
        attn = jnp.einsum('bcj,bij->bci', v, w).reshape(B, C, H, W)
        out = conv1x1(attn, wp, bp)
        return x + out

    def _L1_conv_ref(x, squeeze_w, squeeze_b, expand1x1_w, expand1x1_b, expand3x3_w, expand3x3_b):
        import jax, jax.numpy as jnp
        import numpy as np
        s = jax.nn.relu(jnp.einsum('oc,nchw->nohw', squeeze_w, x) + squeeze_b[None, :, None, None])
        e1 = jax.nn.relu(jnp.einsum('oc,nchw->nohw', expand1x1_w, s) + expand1x1_b[None, :, None, None])
        e3 = jax.lax.conv_general_dilated(s, expand3x3_w, window_strides=(1, 1), padding=((1, 1), (1, 1)), dimension_numbers=('NCHW', 'OIHW', 'NCHW'))
        e3 = jax.nn.relu(e3 + expand3x3_b[None, :, None, None])
        return jnp.concatenate([e1, e3], axis=1)

    def _L2_attn_ref(x, Wq, Wk, Wv, Wo):
        import jax, jax.numpy as jnp
        import numpy as np
        NHEAD = 8
        WINDOW = 64

        def _sliding_window_attention(q, k, v, w):
            B, H, S, D = q.shape
            assert S % w == 0
            nb = S // w
            qb = q.reshape(B, H, nb, w, D)
            kb = k.reshape(B, H, nb, w, D)
            vb = v.reshape(B, H, nb, w, D)
            k_prev = jnp.pad(kb, ((0, 0), (0, 0), (1, 0), (0, 0), (0, 0)))[:, :, :nb]
            v_prev = jnp.pad(vb, ((0, 0), (0, 0), (1, 0), (0, 0), (0, 0)))[:, :, :nb]
            k2 = jnp.concatenate([k_prev, kb], axis=3)
            v2 = jnp.concatenate([v_prev, vb], axis=3)
            scores = jnp.einsum('bhnqd,bhnkd->bhnqk', qb, k2) / jnp.sqrt(jnp.asarray(D, q.dtype))
            qi = jnp.arange(w)[:, None]
            ki = jnp.arange(2 * w)[None, :]
            valid = (ki >= qi + 1) & (ki <= qi + w)
            n_idx = jnp.arange(nb)[:, None, None]
            valid = valid[None] & ((n_idx > 0) | (ki[None] >= w))
            neg = jnp.asarray(-1e+30, scores.dtype)
            scores = jnp.where(valid[None, None], scores, neg)
            attn = jax.nn.softmax(scores, axis=-1)
            out = jnp.einsum('bhnqk,bhnkd->bhnqd', attn, v2)
            return out.reshape(B, H, S, D)
        B, S, Dm = x.shape
        hd = Dm // NHEAD
        q = (x @ Wq.T).reshape(B, S, NHEAD, hd).transpose(0, 2, 1, 3)
        k = (x @ Wk.T).reshape(B, S, NHEAD, hd).transpose(0, 2, 1, 3)
        v = (x @ Wv.T).reshape(B, S, NHEAD, hd).transpose(0, 2, 1, 3)
        attn = _sliding_window_attention(q, k, v, WINDOW)
        attn = attn.transpose(0, 2, 1, 3).reshape(B, S, Dm)
        return attn @ Wo.T

    def _L2_ffn_ref(x, weight, bias):
        import jax, jax.numpy as jnp
        import numpy as np
        IN_FEATURES = 128
        FEATURES = 128
        BATCH, SEQ = (8, 2048)

        def _ste(x_orig, y_proc):
            return x_orig + jax.lax.stop_gradient(y_proc - x_orig)
        weight_centered = weight - jnp.mean(weight)
        weight_bin = jnp.sign(weight_centered)
        weight_bin_ste = _ste(weight, weight_bin)
        scale_gamma = jnp.mean(jnp.abs(weight))
        effective_weight = weight_bin_ste * scale_gamma
        y = jnp.dot(x, effective_weight) + bias
        act_clipped = jnp.clip(y, -1.0, 1.0)
        quant_dequant = jnp.round(act_clipped * 7.0) / 7.0
        return _ste(y, quant_dequant)

    def _L3_attn_ref(x, W_K, W_Q, W_V, W_O):
        import jax, jax.numpy as jnp
        import numpy as np
        D_HEAD = 16
        s = x.shape[-2]
        k = jnp.einsum('ihd,bpd->biph', W_K, x)
        q = jnp.einsum('ihd,bpd->biph', W_Q, x)
        v = jnp.einsum('ihd,bpd->biph', W_V, x)
        scores = jnp.einsum('biph,biqh->biqp', k, q)
        mask = jnp.tril(jnp.ones((s, s), dtype=scores.dtype))
        scores = jnp.tril(scores) - 10000000000.0 * (1.0 - mask)
        attn = jax.nn.softmax(scores / np.sqrt(D_HEAD), axis=-1)
        z = jnp.einsum('biph,biqp->biqh', v, attn)
        b, i, qlen, h = z.shape
        z_flat = jnp.transpose(z, (0, 2, 1, 3)).reshape(b, qlen, i * h)
        out = jnp.einsum('df,bqf->bqd', W_O, z_flat)
        return out

    def _L3_ffn_ref(x, W_router, W1, b1, W2, b2):
        import jax, jax.numpy as jnp
        import numpy as np
        TOP_K = 2
        B, T, C = x.shape
        E = W_router.shape[1]
        x_flat = x.reshape(B * T, C)
        logits = x_flat @ W_router
        probs = jax.nn.softmax(logits, axis=-1)
        topk_p, topk_i = jax.lax.top_k(probs, TOP_K)
        topk_p = topk_p / topk_p.sum(axis=-1, keepdims=True)
        combine = (jax.nn.one_hot(topk_i, E, dtype=x_flat.dtype) * topk_p[..., None]).sum(axis=1)
        out = jnp.zeros_like(x_flat)
        for e in range(E):
            h = jax.nn.relu(x_flat @ W1[e] + b1[e])
            y = h @ W2[e] + b2[e]
            out = out + combine[:, e:e + 1] * y
        return out.reshape(B, T, C)

    def _gn(v, G=32, eps=1e-05):
        B_, C_, H_, W_ = v.shape
        g = v.reshape(B_, G, C_ // G, H_, W_)
        m = jnp.mean(g, axis=(2, 3, 4), keepdims=True)
        s = jnp.var(g, axis=(2, 3, 4), keepdims=True)
        return ((g - m) / jnp.sqrt(s + eps)).reshape(v.shape)

    def _ln_c(v, eps=1e-06):
        m = jnp.mean(v, axis=1, keepdims=True)
        s = jnp.var(v, axis=1, keepdims=True)
        return (v - m) / jnp.sqrt(s + eps)

    def _ln_t(v, eps=1e-05):
        m = jnp.mean(v, axis=-1, keepdims=True)
        s = jnp.var(v, axis=-1, keepdims=True)
        return (v - m) / jnp.sqrt(s + eps)

    def _to_tokens(v):
        B_, C_, H_, W_ = v.shape
        return v.reshape(B_, C_, H_ * W_).transpose(0, 2, 1)

    def _from_tokens(t, like):
        B_, C_, H_, W_ = like.shape
        return t.transpose(0, 2, 1).reshape(B_, C_, H_, W_)
    x = _L0_conv_ref(x, L0_conv_norm_gamma, L0_conv_norm_beta, L0_conv_wq, L0_conv_bq, L0_conv_wk, L0_conv_bk, L0_conv_wv, L0_conv_bv, L0_conv_wp, L0_conv_bp)
    x = x + _L1_conv_ref(_gn(x), L1_conv_squeeze_w, L1_conv_squeeze_b, L1_conv_expand1x1_w, L1_conv_expand1x1_b, L1_conv_expand3x3_w, L1_conv_expand3x3_b)
    t = _to_tokens(x)
    t = t + _L2_attn_ref(_ln_t(t), L2_attn_Wq, L2_attn_Wk, L2_attn_Wv, L2_attn_Wo)
    t = t + _L2_ffn_ref(_ln_t(t), L2_ffn_weight, L2_ffn_bias)
    t = t + _L3_attn_ref(_ln_t(t), L3_attn_W_K, L3_attn_W_Q, L3_attn_W_V, L3_attn_W_O)
    t = t + _L3_ffn_ref(_ln_t(t), L3_ffn_W_router, L3_ffn_W1, L3_ffn_b1, L3_ffn_W2, L3_ffn_b2)
    x = _from_tokens(t, x)
    return x

_drawn_inputs = setup_inputs


def setup_inputs(seed=0):
    import zlib

    import numpy as np

    out = dict(_drawn_inputs(seed))
    spreads = {'L0_conv_norm_gamma': (1.0, 0.2),
     'L0_conv_norm_beta': (0.0, 0.1),
     'L0_conv_bq': (0.0, 0.1),
     'L0_conv_bk': (0.0, 0.8),
     'L0_conv_bv': (0.0, 0.1),
     'L0_conv_bp': (0.0, 0.1),
     'L2_ffn_bias': (0.0, 0.1),
     'L3_ffn_b1': (0.0, 0.456),
     'L3_ffn_b2': (0.0, 0.1)}
    factors = {'L1_conv_squeeze_b': 2.694, 'L2_attn_Wq': 8.0, 'L2_attn_Wk': 8.0}
    for name, (base, spread) in spreads.items():
        noise = np.random.default_rng([zlib.crc32(name.encode()), seed]).standard_normal(out[name].shape)
        drawn = base * np.exp(spread * noise) if base else spread * noise
        out[name] = jnp.asarray(drawn.astype(out[name].dtype))
    for name, factor in factors.items():
        out[name] = (out[name] * factor).astype(out[name].dtype)
    return out
```

```python
from contextlib import ExitStack

import concourse.bass as bass
from concourse import mybir

ALU = mybir.AluOpType
ACT = mybir.ActivationFunctionType
AX = mybir.AxisListType
F32 = mybir.dt.float32
BF16 = mybir.dt.bfloat16
U32 = mybir.dt.uint32

C = 128
B, HH, WW = 4, 16, 16
T = HH * WW
TT = T // 128
NT = B * TT
HEADS, HD = 8, 16
HP = 32
HG = 4
SQ = 16
PW = WW + 2
E, HID = 8, 512
HC = HID // 128
PAIRS = B // 2
UNITS = 6
NEG = -1e30
ROUND = 1.5 * 2.0 ** 23

WIDTHS = dict(
    ident=128, group=128, wq=128, wk=128, wv=128, wp=128, vecs=8, squeeze=96, conv=3 * 128,
    aq=128, ak=128, av=128, ao=256, band0=512, band1=512, fw=128, fb=256, mean=128,
    cq=128, ck=128, cv=128, co=256, causal0=512, causal1=512, headmask=8, router=8, b2=128,
    iota=8,
)
AT = {}
_at = 0
for _name, _width in WIDTHS.items():
    AT[_name] = _at
    _at += _width
PACKED = _at
EARLY = AT["aq"]
GAMMA, BETA, BQ, BK, BV, BP, BSQ, BCONV = range(8)


def build(nc, x, packed, b1, w1, w2, out):
    with ExitStack() as ctx:
        def sb(name, shape, dt=F32):
            return ctx.enter_context(nc.sbuf_tensor(name, shape, dt))

        def pair(name, shape, dt=F32):
            return [sb(f"{name}{p}", shape, dt) for p in range(2)]

        def sem(name):
            return ctx.enter_context(nc.semaphore(name))

        def sems(name):
            return [sem(f"{name}{p}") for p in range(2)]

        bank = [ctx.enter_context(nc.psum_tensor(f"bank{i}", [128, 512], F32)) for i in range(8)]
        bk = [bank[0:4], bank[4:8]]

        pk = sb("pk", [128, PACKED])

        def const(name, lo=0, hi=None):
            return pk[:, AT[name] + lo:AT[name] + (WIDTHS[name] if hi is None else hi)]

        def vec(i):
            return pk[:, AT["vecs"] + i:AT["vecs"] + i + 1]

        ident = const("ident")
        ident_bf = sb("ident_bf", [128, 128], BF16)
        masks_bf = {n: sb(f"{n}_bf", [128, 512], BF16) for n in ("band0", "band1", "causal0", "causal1")}
        neghalf = sb("neghalf", [128, 2])
        carried = sb("carried", [128, 1])
        bq_scaled = sb("bq_scaled", [128, 1])
        w_sum = sb("w_sum", [128, 2])
        w_mean = sb("w_mean", [128, 2])
        w_less = sb("w_less", [128, 128])
        w_eff = sb("w_eff", [128, 128])

        xs = pair("xs", [128, T])
        stats = pair("stats", [128, TT, 6])
        mv = pair("mv", [128, TT, 2])
        gmv = pair("gmv", [128, 2])
        gsq = pair("gsq", [128, 1])
        ve = pair("ve", [128, TT])
        rstd = pair("rstd", [128, TT])
        ga = pair("ga", [128, 1])
        gb = pair("gb", [128, 1])
        hn = pair("hn", [128, T])
        q = pair("q", [128, T])
        k = pair("k", [128, T])
        v0 = pair("v0", [128, T])
        negmax = pair("negmax", [128, 2, HEADS])
        sums = pair("sums", [128, 2, HEADS])
        rinv = pair("rinv", [128, 2])
        prob = pair("prob", [128, 2, 512])
        probT = pair("probT", [128, 2, 512])
        at0 = pair("at0", [128, T])
        x1 = pair("x1", [128, T])
        spad = pair("spad", [96, HH + 2, PW])
        conv_out = pair("conv_out", [128, T])
        t = pair("t", [128, TT, 128])
        ht = pair("ht", [128, TT, 128])
        hT = pair("hT", [128, T])
        kM = pair("kM", [128, HEADS, T])
        vh = pair("vh", [128, TT, HEADS, HP])
        rb = pair("rb", [128, TT, HEADS, HP])
        rT = pair("rT", [128, 512])
        attnT = pair("attnT", [128, HG, 128])
        fy = pair("fy", [128, TT, 128])
        fz = pair("fz", [128, TT, 128])
        fq = pair("fq", [128, TT, 128])
        hT_all = sb("hT_all", [128, B * T])
        t_all = sb("t_all", [128, NT, 128])
        lg = sb("lg", [128, NT, E])
        top = sb("top", [128, NT, 8])
        topi = sb("topi", [128, NT, 8], U32)
        topf = sb("topf", [128, NT, 2])
        gap = sb("gap", [128, NT])
        den = sb("den", [128, NT])
        gate = sb("gate", [128, NT, 2])
        oneh = sb("oneh", [128, NT, E])
        comb = sb("comb", [128, NT, E])
        combT = sb("combT", [E, B * T])
        w1s = pair("w1s", [128, HID])
        b1s = pair("b1s", [128, HC])
        w2s = pair("w2s", [128, HC, 128])
        hb = pair("hb", [128, HC, 512])
        o_sb = sb("o_sb", [128, B * T])

        consts_in, consts2_in = sem("consts_in"), sem("consts2_in")
        x_in = sems("x_in")
        w_in = [sem("w_in0"), sem("w_in1")]
        out_stored = sem("out_stored")
        dve_step = sem("dve_step")
        dve_pre = sem("dve_pre")
        dve_post = sem("dve_post")
        pool_pre = sem("pool_pre")
        act_pre = sem("act_pre")
        casts_ready = sem("casts_ready")
        w_sums_ready, w_means_ready, w_eff_ready = sem("w_sums_ready"), sem("w_means_ready"), sem("w_eff_ready")
        cs_ready, gs_ready, ve_ready, rstd_ready, hn_ready = (
            sems(n) for n in ("cs_ready", "gs_ready", "ve_ready", "rstd_ready", "hn_ready"))
        qk_full, v_full = sems("qk_full"), sems("v_full")
        q_ready, k_ready, v_ready = sems("q_ready"), sems("k_ready"), sems("v_ready")
        s0_full, max0_ready, exp0_done, p0_ready = sems("s0_full"), sems("max0_ready"), sems("exp0_done"), sems("p0_ready")
        pT0_full, pT0_ready, av0_full, at0_ready = sems("pT0_full"), sems("pT0_ready"), sems("av0_full"), sems("at0_ready")
        proj0_full, x1_ready = sems("proj0_full"), sems("x1_ready")
        sq_full, spad_ready, conv_full, conv_ready, x2_ready = (
            sems("sq_full"), sems("spad_ready"), sems("conv_full"), sems("conv_ready"), sems("x2_ready"))
        tok_full = sems("tok_full")
        ln_ve, ln_rstd, ln_h, lnT_full, lnT_ready = (
            sems(n) for n in ("ln_ve", "ln_rstd", "ln_h", "lnT_full", "lnT_ready"))
        aqkv_full, aq_ready, ak_ready, av_ready, s_full, max_ready, exp_done, pT_full, pT_ready, av_full, rb_ready, \
            rT_full, rT_ready, attn_ready, wo_full, t_ready = (
                sems(n) for n in (
                    "aqkv_full", "aq_ready", "ak_ready", "av_ready", "s_full", "max_ready", "exp_done", "pT_full",
                    "pT_ready", "av_full", "rb_ready", "rT_full", "rT_ready", "attn_ready", "wo_full", "t_ready"))
        ffn_full, fy_ready = sems("ffn_full"), sems("fy_ready")
        lg_full, lg_ready, hT_kept = sems("lg_full"), sems("lg_ready"), sems("hT_kept")
        exp_gap, den_ready = sem("exp_gap"), sem("gap_ready")
        comb_ready, combT_full, combT_ready, bias_full, acc_ready = (
            sem("comb_ready"), sem("combT_full"), sem("combT_ready"), sem("bias_full"), sem("acc_ready"))
        h_full, h_ready, y_full, y_used = sem("h_full"), sem("h_ready"), sem("y_full"), sem("y_used")
        oT_full, o_ready = sem("oT_full"), sem("o_ready")

        A_WQ = [const("aq"), const("cq")]
        A_WK = [const("ak"), const("ck")]
        A_WV = [const("av"), const("cv")]
        A_WO = [const("ao"), const("co")]
        A_MASK = [[masks_bf["band0"], masks_bf["band1"]], [masks_bf["causal0"], masks_bf["causal1"]]]

        def unit_query(u):
            return 0 if u < 2 else 1

        def unit_heads(u):
            return range(4 * u, 4 * u + 4) if u < 2 else range(2 * (u - 2), 2 * (u - 2) + 2)

        block = ctx.enter_context(nc.Block())

        @block.sync
        def _(sp):
            sp.dma_start(pk[:, 0:EARLY], packed[:, 0:EARLY]).then_inc(consts_in, 16)
            with sp.Fori(0, PAIRS) as it:
                for p in range(2):
                    sp.wait_ge(x1_ready[p], it)
                    sp.dma_start(xs[p][:, :], x[bass.ds(it * 2 + p, 1)].rearrange("a c t -> c (a t)")
                                 ).then_inc(x_in[p], 16)
                    
            with sp.Fori(0, E // 2) as it:
                for s in range(2):
                    sp.wait_ge(y_full, it * 4)
                    sp.dma_start(w1s[s][:, :], w1[bass.ds(it * 2 + s, 1)].rearrange("e c h -> c (e h)")
                                 ).then_inc(w_in[s], 16)
                    sp.dma_start(b1s[s][:, :], b1[bass.ds(it * 2 + s, 1)].rearrange("e p j -> p (e j)")
                                 ).then_inc(w_in[s], 16)
                    sp.dma_start(w2s[s][:, :, :], w2[bass.ds(it * 2 + s, 1)].rearrange("e (j p) c -> p (e j) c", p=128)
                                 ).then_inc(w_in[s], 16)
            for h in range(2):
                sp.wait_ge(o_ready, h + 1)
                for b in range(2 * h, 2 * h + 2):
                    sp.dma_start(out[b], o_sb[:, b * T:(b + 1) * T]).then_inc(out_stored, 16)
            sp.wait_ge(out_stored, 16 * B)

        @block.gpsimd
        def _(pool):
            nc.gpsimd.memset(neghalf[:, :], -0.5).then_inc(pool_pre, 1)
            for p in range(2):
                nc.gpsimd.memset(spad[p][:, :, :], 0.0).then_inc(pool_pre, 1)
                nc.gpsimd.memset(vh[p][:, :, :, :], 0.0).then_inc(pool_pre, 1)
            pool.wait_ge(pool_pre, 5)

            def power(value, ready, done, n):
                for p in range(2):
                    pool.wait_ge(ready[p], value)
                    nc.gpsimd.tensor_tensor(rstd[p][:, 0:n], ve[p][:, 0:n], neghalf[:, 0:n], ALU.pow
                                            ).then_inc(done[p], 1)

            with pool.Fori(0, PAIRS) as it:
                power(it * 2 + 1, ve_ready, rstd_ready, 1)
                power(it * 2 + 2, ve_ready, rstd_ready, 1)
                for p in range(2):
                    pool.wait_ge(conv_ready[p], it + 1)
                    nc.gpsimd.tensor_tensor(x1[p][:, :], x1[p][:, :], conv_out[p][:, :], ALU.add
                                            ).then_inc(x2_ready[p], 1)
                power(it * 4 + 1, ln_ve, ln_rstd, TT)
                power(it * 4 + 2, ln_ve, ln_rstd, TT)
                power(it * 4 + 3, ln_ve, ln_rstd, TT)
                power(it * 4 + 4, ln_ve, ln_rstd, TT)
                for p in range(2):
                    pool.wait_ge(lnT_ready[p], it * 4 + 3 + 1)
                    nc.gpsimd.tensor_copy(hT_all[:, bass.ds(it * (2 * T) + p * T, T)], hT[p][:, :]
                                          ).then_inc(hT_kept[p], 1)

        @block.scalar
        def _(act):
            act.dma_start(pk[:, EARLY:PACKED], packed[:, EARLY:PACKED]).then_inc(consts2_in, 16)
            act.wait_ge(consts_in, 16)
            nc.scalar.activation(bq_scaled[:, :], vec(BQ), ACT.Copy, scale=float(C) ** -0.5).then_inc(act_pre, 1)
            act.wait_ge(act_pre, 1)
            act.wait_ge(pool_pre, 5)

            def attention(it, a):
                for p in range(2):
                    act.wait_ge(aqkv_full[p], it * 2 + a + 1)
                    nc.scalar.activation(q[p][:, :], bk[p][0][:, 0:T], ACT.Copy, scale=float(HD) ** -0.5
                                         ).then_inc(aq_ready[p], 1)
                    nc.scalar.activation(
                        vh[p][:, :, :, 0:HD],
                        bk[p][2][:, 0:T].rearrange("k (t h d) -> k t h d", t=TT, h=HEADS), ACT.Copy
                    ).then_inc(av_ready[p], 1)
                for u in range(UNITS + 1):
                    for p in range(2):
                        if u < UNITS:
                            act.wait_ge(max_ready[p], (it * 2 + a) * UNITS + u + 1)
                            if u >= 2:
                                act.wait_ge(pT_full[p], (it * 2 + a) * UNITS + u - 1)
                            width = 128 if u < 2 else 256
                            for i, h in enumerate(unit_heads(u)):
                                last = nc.scalar.activation(
                                    prob[p][:, u % 2, i * width:(i + 1) * width],
                                    bk[p][u % 2][:, i * width:(i + 1) * width], ACT.Exp,
                                    bias=negmax[p][:, unit_query(u), h:h + 1],
                                    accum_out=sums[p][:, unit_query(u), h:h + 1])
                            last.then_inc(exp_done[p], 1)
                        if u >= 1 and (u - 1) % 2 == 1:
                            act.wait_ge(pT_full[p], (it * 2 + a) * UNITS + u)
                            nc.scalar.activation(probT[p][:, (u - 1) % 2, :], bk[p][2][:, :], ACT.Copy
                                                 ).then_inc(pT_ready[p], 1)
                for p in range(2):
                    act.wait_ge(rT_full[p], it * 2 + a + 1)
                    nc.scalar.activation(rT[p][:, :], bk[p][2][:, :], ACT.Copy).then_inc(rT_ready[p], 1)

            def turned(it, j, b):
                for p in range(2):
                    act.wait_ge(lnT_full[p], it * 4 + j + 1)
                    nc.scalar.activation(hT[p][:, :], bk[p][b][:, 0:T], ACT.Copy).then_inc(lnT_ready[p], 1)

            with act.Fori(0, PAIRS) as it:
                for p in range(2):
                    act.wait_ge(qk_full[p], it + 1)
                    nc.scalar.activation(q[p][:, :], bk[p][0][:, 0:T], ACT.Identity, bias=bq_scaled[:, :],
                                         scale=float(C) ** -0.5).then_inc(q_ready[p], 1)
                    nc.scalar.activation(k[p][:, :], bk[p][0][:, T:2 * T], ACT.Identity, bias=vec(BK)
                                         ).then_inc(k_ready[p], 1)
                for p in range(2):
                    act.wait_ge(max0_ready[p], it + 1)
                    for i in range(TT):
                        last = nc.scalar.activation(
                            prob[p][:, 0, i * T:(i + 1) * T], bk[p][2][:, i * T:(i + 1) * T], ACT.Exp,
                            bias=negmax[p][:, 0, i:i + 1], accum_out=sums[p][:, 0, i:i + 1])
                    last.then_inc(exp0_done[p], 1)
                for p in range(2):
                    act.wait_ge(pT0_full[p], it + 1)
                    nc.scalar.activation(probT[p][:, 0, :], bk[p][3][:, :], ACT.Copy).then_inc(pT0_ready[p], 1)
                for p in range(2):
                    act.wait_ge(av0_full[p], it + 1)
                    nc.scalar.activation(at0[p][:, :], bk[p][0][:, 0:T], ACT.Identity, bias=vec(BV)
                                         ).then_inc(at0_ready[p], 1)
                for p in range(2):
                    act.wait_ge(sq_full[p], it + 1)
                    for g in range(3):
                        last = nc.scalar.activation(
                            spad[p][32 * g:32 * g + 32, 1:HH + 1, 2 - g:2 - g + WW],
                            bk[p][3][32 * g:32 * g + 32, 0:T].rearrange("c (y x) -> c y x", y=HH), ACT.Relu,
                            bias=vec(BSQ)[32 * g:32 * g + 32, :])
                    last.then_inc(spad_ready[p], 1)
                for p in range(2):
                    act.wait_ge(conv_full[p], it + 1)
                    nc.scalar.activation(conv_out[p][:, :], bk[p][0][:, 0:T], ACT.Relu, bias=vec(BCONV)
                                         ).then_inc(conv_ready[p], 1)
                turned(it, 0, 3)
                attention(it, 0)
                turned(it, 1, 1)
                turned(it, 2, 3)
                attention(it, 1)
                for p in range(2):
                    act.wait_ge(hT_kept[p], it)
                turned(it, 3, 1)

            act.wait_ge(den_ready, 1)
            nc.scalar.activation(gap[:, :], gap[:, :], ACT.Exp).then_inc(exp_gap, 1)
            act.wait_ge(combT_full, 1)
            for h in range(2):
                last = nc.scalar.activation(combT[:, h * 512:(h + 1) * 512], bank[6 + h][0:E, :], ACT.Copy)
            last.then_inc(combT_ready, 1)
            with act.Fori(0, E // 2) as it:
                for s in range(2):
                    for h in range(2):
                        i = 2 * s + h
                        if i >= 2:
                            act.wait_ge(y_full, it * 4 + i - 1)
                        elif i == 0:
                            act.wait_ge(y_full, it * 4)
                        for j in range(HC):
                            act.wait_ge(h_full, it * (4 * HC) + i * HC + j + 1)
                            nc.scalar.activation(
                                hb[i % 2][:, j, :], bank[j][:, :], ACT.Relu,
                                bias=b1s[s][:, j:j + 1]
                            ).then_inc(h_ready, 1)
            for h in range(2):
                act.wait_ge(oT_full, h + 1)
                nc.scalar.activation(o_sb[:, h * 512:(h + 1) * 512], bank[h][:, :], ACT.Copy).then_inc(o_ready, 1)

        @block.tensor
        def _(pe):
            mm = nc.tensor.matmul

            pe.wait_ge(w_sums_ready, 1)
            mm(bank[7][:, 0:2], const("mean"), w_sum[:, :], start=True, stop=True).then_inc(w_means_ready, 1)
            pe.wait_ge(casts_ready, 5)
            pe.wait_ge(w_eff_ready, 1)
            pe.wait_ge(pool_pre, 5)

            def turn(it, j, b):
                for p in range(2):
                    pe.wait_ge(ln_h[p], it * 4 + j + 1)
                    for i in range(TT):
                        last = nc.tensor.transpose(bk[p][b][:, i * 128:(i + 1) * 128], ht[p][:, i, :], ident)
                    last.then_inc(lnT_full[p], 1)

            def scores(it, a, p, u):
                if u == 0:
                    pe.wait_ge(aq_ready[p], it * 2 + a + 1)
                    pe.wait_ge(ak_ready[p], it * 2 + a + 1)
                if u >= 2:
                    pe.wait_ge(exp_done[p], (it * 2 + a) * UNITS + u - 1)
                width = 128 if u < 2 else 256
                i = unit_query(u)
                dst = bk[p][u % 2]
                mm(dst[:, :], ident_bf[:, :], A_MASK[a][i][:, :], start=True, stop=False, skip_group_check=True)
                for n, h in enumerate(unit_heads(u)):
                    last = mm(dst[:, n * width:(n + 1) * width], q[p][:, i * 128:(i + 1) * 128],
                              kM[p][:, h, 0:width], start=False, stop=True, skip_group_check=True)
                last.then_inc(s_full[p], 1)

            def turn_probs(it, a, p, u):
                pe.wait_ge(exp_done[p], (it * 2 + a) * UNITS + u + 1)
                if u == 0:
                    pe.wait_ge(av_ready[p], it * 2 + a + 1)
                else:
                    pe.wait_ge(pT_ready[p], (it * 2 + a) * UNITS + u)
                for n in range(4):
                    last = nc.tensor.transpose(bk[p][2][:, n * 128:(n + 1) * 128],
                                               prob[p][:, u % 2, n * 128:(n + 1) * 128], ident)
                last.then_inc(pT_full[p], 1)

            def mix(it, a, p, u):
                pe.wait_ge(pT_ready[p], (it * 2 + a) * UNITS + u + 1)
                tiles = 1 if u < 2 else 2
                for kt in range(tiles):
                    for n, h in enumerate(unit_heads(u)):
                        g, r = divmod(h, HG)
                        col = (2 * g + unit_query(u)) * 128
                        last = mm(bk[p][3][HP * r:HP * r + HP, col:col + 128], vh[p][:, kt, h, :],
                                  probT[p][:, u % 2, (n * tiles + kt) * 128:(n * tiles + kt + 1) * 128],
                                  start=(kt == 0), stop=(kt == tiles - 1), tile_position=(0, HP * r))
                if u == UNITS - 1:
                    last.then_inc(av_full[p], 1)

            def attention(it, a):
                for p in range(2):
                    pe.wait_ge(lnT_ready[p], it * 4 + 2 * a + 1)
                    mm(bk[p][0][:, 0:T], A_WQ[a], hT[p][:, :], start=True, stop=True)
                    mm(bk[p][1][:, 0:T], A_WK[a], hT[p][:, :], start=True, stop=True)
                    for i in range(TT):
                        last = mm(bk[p][2][:, i * 128:(i + 1) * 128], hT[p][:, i * 128:(i + 1) * 128], A_WV[a],
                                  start=True, stop=True)
                    last.then_inc(aqkv_full[p], 1)
                for u in range(UNITS + 2):
                    for p in range(2):
                        if u < UNITS:
                            scores(it, a, p, u)
                        if 1 <= u <= UNITS:
                            turn_probs(it, a, p, u - 1)
                        if u >= 2:
                            mix(it, a, p, u - 2)
                for p in range(2):
                    pe.wait_ge(rb_ready[p], it * 2 + a + 1)
                    for g in range(2):
                        for i in range(TT):
                            col = (2 * g + i) * 128
                            last = nc.tensor.transpose(
                                bk[p][2][:, col:col + 128],
                                rb[p][:, i, HG * g:HG * g + HG, :].rearrange("q h d -> q (h d)"), ident)
                    last.then_inc(rT_full[p], 1)
                for p in range(2):
                    pe.wait_ge(attn_ready[p], it * 2 + a + 1)
                    for i in range(TT):
                        for g in range(2):
                            last = mm(bk[p][0][:, i * 128:(i + 1) * 128], attnT[p][:, 2 * g + i, :],
                                      A_WO[a][:, g * 128:(g + 1) * 128], start=(g == 0), stop=(g == 1))
                    last.then_inc(wo_full[p], 1)

            def group_stats(it, j, b):
                for p in range(2):
                    pe.wait_ge(cs_ready[p], it * 2 + j + 1)
                    mm(bk[p][b][:, 0:2], const("group"), mv[p][:, 0, :], start=True, stop=True
                       ).then_inc(gs_ready[p], 1)

            with pe.Fori(0, PAIRS) as it:
                group_stats(it, 0, 3)
                for p in range(2):
                    pe.wait_ge(hn_ready[p], it * 2 + 0 + 1)
                    mm(bk[p][0][:, 0:T], const("wq"), hn[p][:, :], start=True, stop=True)
                    mm(bk[p][0][:, T:2 * T], const("wk"), hn[p][:, :], start=True, stop=True
                       ).then_inc(qk_full[p], 1)
                    for i in range(TT):
                        last = mm(bk[p][1][:, i * 128:(i + 1) * 128], hn[p][:, i * 128:(i + 1) * 128], const("wv"),
                                  start=True, stop=True)
                    last.then_inc(v_full[p], 1)
                for p in range(2):
                    pe.wait_ge(q_ready[p], it + 1)
                    pe.wait_ge(k_ready[p], it + 1)
                    pe.wait_ge(lg_ready[p], it)
                    for i in range(TT):
                        last = mm(bk[p][2][:, i * T:(i + 1) * T], q[p][:, i * 128:(i + 1) * 128], k[p][:, :],
                                  start=True, stop=True)
                    last.then_inc(s0_full[p], 1)
                for p in range(2):
                    pe.wait_ge(p0_ready[p], it + 1)
                    for kt in range(TT):
                        for i in range(TT):
                            last = nc.tensor.transpose(
                                bk[p][3][:, kt * T + i * 128:kt * T + (i + 1) * 128],
                                prob[p][:, 0, i * T + kt * 128:i * T + (kt + 1) * 128], ident)
                    last.then_inc(pT0_full[p], 1)
                for p in range(2):
                    pe.wait_ge(pT0_ready[p], it + 1)
                    pe.wait_ge(v_ready[p], it + 1)
                    for kt in range(TT):
                        last = mm(bk[p][0][:, 0:T], v0[p][:, kt * 128:(kt + 1) * 128],
                                  probT[p][:, 0, kt * T:(kt + 1) * T], start=(kt == 0), stop=(kt == TT - 1))
                    last.then_inc(av0_full[p], 1)
                for p in range(2):
                    pe.wait_ge(at0_ready[p], it + 1)
                    mm(bk[p][1][:, 0:T], const("wp"), at0[p][:, :], start=True, stop=True).then_inc(proj0_full[p], 1)
                group_stats(it, 1, 2)
                for p in range(2):
                    pe.wait_ge(hn_ready[p], it * 2 + 1 + 1)
                    mm(bk[p][3][0:96, 0:T], const("squeeze"), hn[p][:, :], start=True, stop=True
                       ).then_inc(sq_full[p], 1)
                for p in range(2):
                    pe.wait_ge(spad_ready[p], it + 1)
                    for dy in range(3):
                        last = mm(bk[p][0][:, 0:T], const("conv")[0:96, dy * 128:(dy + 1) * 128],
                                  spad[p][:, dy:dy + HH, 1:1 + WW], start=(dy == 0), stop=(dy == 2))
                    last.then_inc(conv_full[p], 1)
                for p in range(2):
                    pe.wait_ge(x2_ready[p], it + 1)
                    for i in range(TT):
                        last = nc.tensor.transpose(bk[p][1][:, i * 128:(i + 1) * 128],
                                                   x1[p][:, i * 128:(i + 1) * 128], ident)
                    last.then_inc(tok_full[p], 1)
                turn(it, 0, 3)
                attention(it, 0)
                turn(it, 1, 1)
                for p in range(2):
                    pe.wait_ge(lnT_ready[p], it * 4 + 1 + 1)
                    for i in range(TT):
                        last = mm(bk[p][2][:, i * 128:(i + 1) * 128], hT[p][:, i * 128:(i + 1) * 128], w_eff[:, :],
                                  start=True, stop=True)
                    last.then_inc(ffn_full[p], 1)
                turn(it, 2, 3)
                attention(it, 1)
                turn(it, 3, 1)
                for p in range(2):
                    pe.wait_ge(lnT_ready[p], it * 4 + 3 + 1)
                    for i in range(TT):
                        last = mm(bk[p][2][:, i * E:(i + 1) * E], hT[p][:, i * 128:(i + 1) * 128], const("router"),
                                  start=True, stop=True)
                    last.then_inc(lg_full[p], 1)

            pe.wait_ge(comb_ready, 1)
            for i in range(NT):
                last = nc.tensor.transpose(bank[6 + i // 4][0:E, (i % 4) * 128:(i % 4 + 1) * 128], comb[:, i, :], ident)
            last.then_inc(combT_full, 1)
            pe.wait_ge(combT_ready, 1)
            for i in range(NT):
                last = mm(bank[4 + i // 4][:, (i % 4) * 128:(i % 4 + 1) * 128], combT[:, i * 128:(i + 1) * 128],
                          const("b2")[0:E, :], start=True, stop=True)
            last.then_inc(bias_full, 1)
            for p in range(2):
                pe.wait_ge(hT_kept[p], PAIRS)
            pe.wait_ge(acc_ready, 1)

            def hidden(it, i):
                s, h = divmod(i, 2)
                if h == 0:
                    pe.wait_ge(w_in[s], it * 48 + 48)
                for j in range(HC):
                    pe.wait_ge(h_ready, it * (4 * HC) + i * HC + j + 1 - HC) if i else pe.wait_ge(h_ready, it * (4 * HC))
                    mm(bank[j][:, :], w1s[s][:, j * 128:(j + 1) * 128], hT_all[:, h * 512:(h + 1) * 512],
                       start=True, stop=True).then_inc(h_full, 1)

            def down(it, i):
                s, h = divmod(i, 2)
                pe.wait_ge(h_ready, it * (4 * HC) + i * HC + HC)
                pe.wait_ge(y_used, it * 4 + i - 1) if i >= 2 else pe.wait_ge(y_used, it * 4)
                for n in range(4):
                    for j in range(HC):
                        last = mm(bank[4 + i % 2][:, n * 128:(n + 1) * 128], hb[i % 2][:, j, n * 128:(n + 1) * 128],
                                  w2s[s][:, j, :], start=(j == 0), stop=(j == HC - 1))
                last.then_inc(y_full, 1)

            with pe.Fori(0, E // 2) as it:
                hidden(it, 0)
                for i in range(4):
                    if i < 3:
                        hidden(it, i + 1)
                    down(it, i)
            pe.wait_ge(y_used, 2 * E)
            for h in range(2):
                for n in range(4):
                    last = nc.tensor.transpose(bank[h][:, n * 128:(n + 1) * 128], t_all[:, 4 * h + n, :], ident)
                last.then_inc(oT_full, 1)

        @block.vector
        def _(dve):
            V = nc.vector
            pre = [0]

            def then(ins):
                pre[0] += 1
                ins.then_inc(dve_pre, 1)
                dve.wait_ge(dve_pre, pre[0])

            dve.wait_ge(consts_in, 16)
            dve.wait_ge(consts2_in, 16)
            V.tensor_copy(ident_bf[:, :], ident).then_inc(casts_ready, 1)
            for name, mask in masks_bf.items():
                V.tensor_copy(mask[:, :], const(name)).then_inc(casts_ready, 1)
            V.tensor_reduce(w_sum[:, 0:1], const("fw"), AX.X, ALU.add)
            V.tensor_reduce(w_sum[:, 1:2], const("fw"), AX.X, ALU.add, apply_absolute_value=True
                            ).then_inc(w_sums_ready, 1)
            dve.wait_ge(w_means_ready, 1)
            then(V.tensor_copy(w_mean[:, :], bank[7][:, 0:2]))
            V.tensor_scalar(w_less[:, :], const("fw"), w_mean[:, 0:1], None, ALU.is_lt)
            then(V.tensor_scalar(w_eff[:, :], const("fw"), w_mean[:, 0:1], None, ALU.is_gt))
            then(V.tensor_tensor(w_eff[:, :], w_eff[:, :], w_less[:, :], ALU.subtract))
            then(V.tensor_tensor(w_eff[:, :], w_eff[:, :], const("fw"), ALU.subtract))
            then(V.tensor_tensor(w_eff[:, :], w_eff[:, :], const("fw"), ALU.add))
            V.tensor_scalar(w_eff[:, :], w_eff[:, :], w_mean[:, 1:2], None, ALU.mult).then_inc(w_eff_ready, 1)

            count = [0]

            def step(it, ins, carrier=None):
                count[0] += 1
                ins.then_inc(dve_step, 1)
                dve.wait_ge(dve_step, it * STEPS + count[0])
                if carrier is not None:
                    V.tensor_copy(carried[:, :], carrier)

            def group_norm(it, j, src, b, eps, affine):
                for p in range(2):
                    if j == 0:
                        dve.wait_ge(x_in[p], it * 16 + 16)
                    step(it, V.bn_stats(stats[p][:, 0, :], src[p][:, :]), stats[p][:, 0, 0:1])
                    step(it, V.bn_aggr(mv[p][:, 0, :], stats[p][:, 0, :]))
                    V.scalar_tensor_tensor(mv[p][:, 0, 1:2], mv[p][:, 0, 0:1], mv[p][:, 0, 0:1], mv[p][:, 0, 1:2],
                                           ALU.mult, ALU.add).then_inc(cs_ready[p], 1)
                for p in range(2):
                    dve.wait_ge(gs_ready[p], it * 2 + j + 1)
                    step(it, V.tensor_copy(gmv[p][:, :], bk[p][b][:, 0:2]))
                    step(it, V.tensor_tensor(gsq[p][:, :], gmv[p][:, 0:1], gmv[p][:, 0:1], ALU.mult))
                    V.scalar_tensor_tensor(ve[p][:, 0:1], gmv[p][:, 1:2], eps, gsq[p][:, :], ALU.add, ALU.subtract
                                           ).then_inc(ve_ready[p], 1)
                for p in range(2):
                    dve.wait_ge(rstd_ready[p], it * 2 + j + 1)
                    if affine:
                        step(it, V.tensor_tensor(ga[p][:, :], rstd[p][:, 0:1], vec(GAMMA), ALU.mult))
                        step(it, V.scalar_tensor_tensor(gb[p][:, :], gmv[p][:, 0:1], ga[p][:, 0:1], vec(BETA),
                                                        ALU.mult, ALU.subtract))
                        V.tensor_scalar(hn[p][:, :], src[p][:, :], ga[p][:, 0:1], gb[p][:, 0:1],
                                        ALU.mult, ALU.subtract).then_inc(hn_ready[p], 1)
                    else:
                        V.tensor_scalar(hn[p][:, :], src[p][:, :], gmv[p][:, 0:1], rstd[p][:, 0:1],
                                        ALU.subtract, ALU.mult).then_inc(hn_ready[p], 1)

            def layer_norm(it, j):
                for p in range(2):
                    for i in range(TT):
                        last = V.bn_stats(stats[p][:, i, :], t[p][:, i, :])
                    step(it, last, stats[p][:, 0, 0:1])
                    for i in range(TT):
                        last = V.bn_aggr(mv[p][:, i, :], stats[p][:, i, :])
                    step(it, last)
                    V.tensor_scalar(ve[p][:, :], mv[p][:, :, 1], 1e-5, None, ALU.add).then_inc(ln_ve[p], 1)
                for p in range(2):
                    dve.wait_ge(ln_rstd[p], it * 4 + j + 1)
                    for i in range(TT):
                        last = V.tensor_scalar(ht[p][:, i, :], t[p][:, i, :], mv[p][:, i, 0:1], rstd[p][:, i:i + 1],
                                               ALU.subtract, ALU.mult)
                    last.then_inc(ln_h[p], 1)

            def attention(it, a):
                for p in range(2):
                    dve.wait_ge(aqkv_full[p], it * 2 + a + 1)
                    step(it, V.tensor_copy(k[p][:, :], bk[p][1][:, 0:T]))
                    for h in range(HEADS):
                        last = V.tensor_scalar(kM[p][:, h, :], k[p][:, :], const("headmask", h, h + 1), None, ALU.mult)
                    last.then_inc(ak_ready[p], 1)
                for u in range(UNITS + 1):
                    for p in range(2):
                        if u < UNITS:
                            dve.wait_ge(s_full[p], (it * 2 + a) * UNITS + u + 1)
                            heads = unit_heads(u)
                            V.tensor_reduce(negmax[p][:, unit_query(u), heads[0]:heads[-1] + 1],
                                            bk[p][u % 2][:, :].rearrange("q (h k) -> q h k", h=len(heads)),
                                            AX.X, ALU.max, negate=True).then_inc(max_ready[p], 1)
                        if u >= 1 and (u - 1) % 2 == 0:
                            dve.wait_ge(pT_full[p], (it * 2 + a) * UNITS + u)
                            V.tensor_copy(probT[p][:, (u - 1) % 2, :], bk[p][2][:, :]).then_inc(pT_ready[p], 1)
                for p in range(2):
                    dve.wait_ge(exp_done[p], (it * 2 + a) * UNITS + UNITS)
                    V.reciprocal(rb[p][:, :, :, :], sums[p][:, :, :].unsqueeze(3).to_broadcast([128, TT, HEADS, HP])
                                 ).then_inc(rb_ready[p], 1)
                for p in range(2):
                    dve.wait_ge(rT_ready[p], it * 2 + a + 1)
                    dve.wait_ge(av_full[p], it * 2 + a + 1)
                    V.tensor_tensor(attnT[p][:, :, :], bk[p][3][:, :].rearrange("d (n q) -> d n q", n=HG),
                                    rT[p][:, :].rearrange("d (n q) -> d n q", n=HG), ALU.mult
                                    ).then_inc(attn_ready[p], 1)
                for p in range(2):
                    dve.wait_ge(wo_full[p], it * 2 + a + 1)
                    step(it, V.tensor_tensor(t[p][:, :, :], bk[p][0][:, 0:T].rearrange("q (i c) -> q i c", i=TT),
                                             t[p][:, :, :], ALU.add))

            def loop_body(it):
                count[0] = 0
                group_norm(it, 0, xs, 3, 1e-6, True)
                for p in range(2):
                    dve.wait_ge(v_full[p], it + 1)
                    V.tensor_copy(v0[p][:, :], bk[p][1][:, 0:T]).then_inc(v_ready[p], 1)
                for p in range(2):
                    dve.wait_ge(s0_full[p], it + 1)
                    V.tensor_reduce(negmax[p][:, 0, 0:TT], bk[p][2][:, :].rearrange("q (i k) -> q i k", i=TT),
                                    AX.X, ALU.max, negate=True).then_inc(max0_ready[p], 1)
                for p in range(2):
                    dve.wait_ge(exp0_done[p], it + 1)
                    step(it, V.reciprocal(rinv[p][:, :], sums[p][:, 0, 0:TT]))
                    for i in range(TT):
                        last = V.tensor_scalar(prob[p][:, 0, i * T:(i + 1) * T], prob[p][:, 0, i * T:(i + 1) * T],
                                               rinv[p][:, i:i + 1], None, ALU.mult)
                    last.then_inc(p0_ready[p], 1)
                for p in range(2):
                    dve.wait_ge(proj0_full[p], it + 1)
                    V.scalar_tensor_tensor(x1[p][:, :], bk[p][1][:, 0:T], vec(BP), xs[p][:, :], ALU.add, ALU.add
                                           ).then_inc(x1_ready[p], 1)
                    dve.wait_ge(x1_ready[p], it + 1)
                group_norm(it, 1, x1, 2, 1e-5, False)
                for p in range(2):
                    dve.wait_ge(tok_full[p], it + 1)
                    step(it, V.tensor_copy(t[p][:, :, :], bk[p][1][:, 0:T].rearrange("q (i c) -> q i c", i=TT)))
                layer_norm(it, 0)
                attention(it, 0)
                layer_norm(it, 1)
                for p in range(2):
                    dve.wait_ge(ffn_full[p], it + 1)
                    step(it, V.tensor_tensor(fy[p][:, :, :], bk[p][2][:, 0:T].rearrange("q (i c) -> q i c", i=TT),
                                             const("fb").rearrange("q (i c) -> q i c", i=TT), ALU.add))
                    step(it, V.tensor_scalar(fz[p][:, :, :], fy[p][:, :, :], -1.0, 1.0, ALU.max, ALU.min))
                    step(it, V.tensor_scalar(fz[p][:, :, :], fz[p][:, :, :], 7.0, ROUND, ALU.mult, ALU.add))
                    step(it, V.tensor_scalar(fz[p][:, :, :], fz[p][:, :, :], ROUND, 1.0 / 7.0, ALU.subtract, ALU.mult))
                    step(it, V.tensor_tensor(fz[p][:, :, :], fz[p][:, :, :], fy[p][:, :, :], ALU.subtract))
                    step(it, V.tensor_tensor(fz[p][:, :, :], fz[p][:, :, :], fy[p][:, :, :], ALU.add))
                    step(it, V.tensor_tensor(t[p][:, :, :], t[p][:, :, :], fz[p][:, :, :], ALU.add))
                layer_norm(it, 2)
                attention(it, 1)
                layer_norm(it, 3)
                for p in range(2):
                    V.tensor_copy(t_all[:, bass.ds(it * (2 * TT) + p * TT, TT), :], t[p][:, :, :])
                    dve.wait_ge(lg_full[p], it + 1)
                    V.tensor_copy(lg[:, bass.ds(it * (2 * TT) + p * TT, TT), :],
                                  bk[p][2][:, 0:TT * E].rearrange("q (i e) -> q i e", i=TT)).then_inc(lg_ready[p], 1)

            STEPS = 62
            with dve.Fori(0, PAIRS) as it:
                loop_body(it)
            assert count[0] == STEPS, count[0]

            post = [0]

            def after(ins):
                post[0] += 1
                ins.then_inc(dve_post, 1)
                dve.wait_ge(dve_post, post[0])

            for p in range(2):
                dve.wait_ge(lg_ready[p], PAIRS)
            for i in range(NT):
                last = V.max(top[:, i, :], lg[:, i, :])
            after(last)
            V.tensor_tensor(gap[:, :], top[:, :, 1], top[:, :, 0], ALU.subtract).then_inc(den_ready, 1)
            for i in range(NT):
                last = V.max_index(topi[:, i, :], top[:, i, :], lg[:, i, :])
            after(last)
            after(V.tensor_copy(topf[:, :, :], topi[:, :, 0:2]))
            dve.wait_ge(exp_gap, 1)
            after(V.tensor_scalar(den[:, :], gap[:, :], 1.0, None, ALU.add))
            after(V.reciprocal(gate[:, :, 0], den[:, :]))
            after(V.tensor_tensor(gate[:, :, 1], gap[:, :], gate[:, :, 0], ALU.mult))

            def wide(ap):
                return ap.unsqueeze(2).to_broadcast([128, NT, E])

            iota = const("iota").unsqueeze(1).to_broadcast([128, NT, E])
            V.tensor_tensor(comb[:, :, :], iota, wide(topf[:, :, 0]), ALU.is_equal)
            after(V.tensor_tensor(oneh[:, :, :], iota, wide(topf[:, :, 1]), ALU.is_equal))
            V.tensor_tensor(comb[:, :, :], comb[:, :, :], wide(gate[:, :, 0]), ALU.mult)
            after(V.tensor_tensor(oneh[:, :, :], oneh[:, :, :], wide(gate[:, :, 1]), ALU.mult))
            V.tensor_tensor(comb[:, :, :], comb[:, :, :], oneh[:, :, :], ALU.add).then_inc(comb_ready, 1)
            dve.wait_ge(bias_full, 1)
            for h in range(2):
                last = V.tensor_tensor(t_all[:, 4 * h:4 * h + 4, :], bank[4 + h][:, :].rearrange("q (i c) -> q i c", i=4),
                                       t_all[:, 4 * h:4 * h + 4, :], ALU.add)
            last.then_inc(acc_ready, 1)
            dve.wait_ge(acc_ready, 1)
            comb_flat = comb[:, :, :].rearrange("q i e -> q (i e)")
            with dve.Fori(0, E // 2) as it:
                for i in range(4):
                    s, h = divmod(i, 2)
                    dve.wait_ge(y_full, it * 4 + i + 1)
                    dve.wait_ge(y_used, it * 4 + i - 1) if i >= 2 else dve.wait_ge(y_used, it * 4)
                    for n in range(4):
                        tile = 4 * h + n
                        last = V.scalar_tensor_tensor(
                            t_all[:, tile, :], bank[4 + i % 2][:, n * 128:(n + 1) * 128],
                            comb_flat[:, bass.ds(it * 2 + (tile * E + s), 1)], t_all[:, tile, :], ALU.mult, ALU.add)
                    last.then_inc(y_used, 1)


def kernel(**inputs):
    import numpy as np
    import concourse.bacc as bacc
    from concourse.bass_utils import run_bass_kernel_spmd

    a = {n: np.asarray(v) for n, v in inputs.items()}
    f32 = np.float32

    def padded_rows(w):
        r = np.zeros((2, HG, HP, 128), f32)
        r[:, :, 0:HD] = w.reshape(2, HG, HD, 128)
        return r.reshape(2, 128, 128).transpose(1, 0, 2).reshape(128, 256)

    def rows(w, n=128):
        r = np.zeros((128, w.shape[1]), f32)
        r[0:w.shape[0]] = w
        return r

    vecs = np.zeros((128, 8), f32)
    for i, n in ((GAMMA, "norm_gamma"), (BETA, "norm_beta"), (BQ, "bq"), (BK, "bk"), (BV, "bv"), (BP, "bp")):
        vecs[:, i] = a["L0_conv_" + n]
    squeeze = np.zeros((128, 96), f32)
    conv = np.zeros((128, 3, 128), f32)
    for g in range(3):
        squeeze[:, 32 * g:32 * g + SQ] = a["L1_conv_squeeze_w"].T
        vecs[32 * g:32 * g + SQ, BSQ] = a["L1_conv_squeeze_b"]
        for dy in range(3):
            conv[32 * g:32 * g + SQ, dy, 64:128] = a["L1_conv_expand3x3_w"][:, :, dy, g].T
    conv[32:32 + SQ, 1, 0:64] = a["L1_conv_expand1x1_w"].T
    vecs[0:64, BCONV] = a["L1_conv_expand1x1_b"]
    vecs[64:128, BCONV] = a["L1_conv_expand3x3_b"]

    qi = np.arange(128)[:, None]
    ki = np.arange(256)[None, :]

    def mask(valid, times):
        return np.tile(np.where(valid, 0.0, NEG).astype(f32), (1, times))

    band = [(ki <= qi + 128 * i) & (ki > qi + 128 * i - 64) for i in range(2)]
    causal = [ki <= qi + 128 * i for i in range(2)]
    ch = np.arange(128)
    parts = dict(
        ident=np.eye(128, dtype=f32), group=(ch[:, None] // 4 == ch[None, :] // 4).astype(f32) * f32(0.25),
        wq=a["L0_conv_wq"].T, wk=a["L0_conv_wk"].T, wv=a["L0_conv_wv"].T, wp=a["L0_conv_wp"].T, vecs=vecs,
        squeeze=squeeze, conv=conv.reshape(128, 384),
        aq=a["L2_attn_Wq"].T, ak=a["L2_attn_Wk"].T, av=a["L2_attn_Wv"].T, ao=padded_rows(a["L2_attn_Wo"].T),
        band0=mask(band[0][:, 0:128], 4), band1=mask(band[1], 2),
        fw=a["L2_ffn_weight"], fb=np.tile(a["L2_ffn_bias"][None, :], (128, 2)), mean=np.full((128, 128), 1.0 / C / C, f32),
        cq=a["L3_attn_W_Q"].reshape(128, 128).T, ck=a["L3_attn_W_K"].reshape(128, 128).T,
        cv=a["L3_attn_W_V"].reshape(128, 128).T, co=padded_rows(a["L3_attn_W_O"].T),
        causal0=mask(causal[0][:, 0:128], 4), causal1=mask(causal[1], 2),
        headmask=(ch[:, None] // HD == np.arange(HEADS)[None, :]).astype(f32), router=a["L3_ffn_W_router"],
        b2=rows(a["L3_ffn_b2"]),
        iota=np.tile(np.arange(8, dtype=f32)[None, :], (128, 1)),
    )
    assert list(parts) == list(WIDTHS)
    packed = np.concatenate([np.ascontiguousarray(parts[n]) for n in parts], axis=1)
    arrays = {
        "x": np.ascontiguousarray(a["x"].reshape(B, C, T)), "packed": packed,
        "b1": np.ascontiguousarray(a["L3_ffn_b1"].reshape(E, HC, 128).transpose(0, 2, 1)),
        "w1": np.ascontiguousarray(a["L3_ffn_W1"]), "w2": np.ascontiguousarray(a["L3_ffn_W2"]),
    }
    nc = bacc.Bacc("TRN2", target_bir_lowering=False, num_devices=1)
    ins = [nc.dram_tensor(n, v.shape, F32, kind="ExternalInput").ap() for n, v in arrays.items()]
    out = nc.dram_tensor("out", (B, C, T), F32, kind="ExternalOutput").ap()
    build(nc, *ins, out)
    r = run_bass_kernel_spmd(nc, [arrays], core_ids=[0])
    return r.results[0]["out"].reshape(B, C, HH, WW)
```

```python
from contextlib import ExitStack

import concourse.bass as bass
from concourse import mybir

ALU = mybir.AluOpType
ACT = mybir.ActivationFunctionType
AX = mybir.AxisListType
F32 = mybir.dt.float32
BF16 = mybir.dt.bfloat16
F32R = mybir.dt.float32r
U32 = mybir.dt.uint32

C = 128
B, HH, WW = 4, 16, 16
T = HH * WW
TT = T // 128
NT = B * TT
HEADS, HD = 8, 16
HP = 32
HG = 4
SQ = 16
PW = WW + 2
E, HID = 8, 512
HC = HID // 128
UNITS = 6
TOK = B * T
BLOCKS = 2 * E
NEG = -1e30
ROUND = 1.5 * 2.0 ** 23

WIDTHS = dict(
    ident=128, group=128, wq=128, wk=128, wv=128, wp=128, vecs=8, squeeze=96, conv=3 * 128,
    aq=128, ak=128, av=128, ao=256, band0=512, band1=512, fw=128, fb=256, mean=128,
    cq=128, ck=128, cv=128, co=256, causal0=512, causal1=512, headmask=8, router=8,
    iota=8,
)
AT = {}
_at = 0
for _name, _width in WIDTHS.items():
    AT[_name] = _at
    _at += _width
PACKED = _at
EARLY = AT["aq"]
GAMMA, BETA, BQ, BK, BV, BP, BSQ, BCONV = range(8)


def build(nc, x, packed, b1, b2, w1, w2, routes, out):
    with ExitStack() as ctx:
        attention_memory = ExitStack()

        def sb(name, shape, dt=F32, scope=ctx):
            return scope.enter_context(nc.sbuf_tensor(name, shape, dt))

        def each(name, shape, dt=F32, n=B, scope=ctx):
            return [sb(f"{name}{i}", shape, dt, scope) for i in range(n)]

        def sem(name):
            return ctx.enter_context(nc.semaphore(name))

        def sems(name, n=B):
            return [sem(f"{name}{i}") for i in range(n)]

        bank = [ctx.enter_context(nc.psum_tensor(f"bank{i}", [128, 512], F32)) for i in range(8)]
        two = [bank[4 * (n % 2) + 2 * (n // 2):][:2] for n in range(B)]
        lane = [bank[4 * (n % 2):][:4] for n in range(B)]

        pk = sb("pk", [128, PACKED])

        def const(name, lo=0, hi=None):
            return pk[:, AT[name] + lo:AT[name] + (WIDTHS[name] if hi is None else hi)]

        def vec(i):
            return pk[:, AT["vecs"] + i:AT["vecs"] + i + 1]

        ident = const("ident")
        ident_bf = sb("ident_bf", [128, 128], BF16)
        masks_bf = {n: sb(f"{n}_bf", [128, 512], BF16) for n in ("band0", "band1", "causal0", "causal1")}
        neghalf = sb("neghalf", [128, 2])
        bq_scaled = sb("bq_scaled", [128, 1])
        w_sum = sb("w_sum", [128, 2])
        w_mean = sb("w_mean", [128, 2])
        w_less = sb("w_less", [128, 128])
        w_eff = sb("w_eff", [128, 128])

        xs = each("xs", [128, T])
        stats = each("stats", [128, TT, 6])
        mv = each("mv", [128, TT, 2])
        gmv = each("gmv", [128, 2])
        gsq = each("gsq", [128, 1])
        ve = each("ve", [128, TT])
        rstd = each("rstd", [128, TT])
        ga = each("ga", [128, 1])
        gb = each("gb", [128, 1])
        hn = each("hn", [128, T])
        q = each("q", [128, T])
        k = each("k", [128, T])
        v0 = each("v0", [128, T])
        negmax = each("negmax", [128, 2, HEADS])
        sums = each("sums", [128, 2, HEADS])
        rinv = each("rinv", [128, 2, HEADS])
        at0 = each("at0", [128, T])
        x1 = each("x1", [128, T])
        spad = each("spad", [96, HH + 2, PW])
        conv_out = each("conv_out", [128, T])
        t = each("t", [128, TT, 128])
        ht = each("ht", [128, TT, 128])
        hT = each("hT", [128, T])
        fy = each("fy", [128, TT, 128])
        fz = each("fz", [128, TT, 128])
        vh = each("vh", [128, TT, HEADS, HP])
        lg = sb("lg", [128, NT, E])
        top = sb("top", [128, NT, 8])
        topi = sb("topi", [128, NT, 8], U32)
        topf = sb("topf", [128, NT, 2])
        gap = sb("gap", [128, NT])
        den = sb("den", [128, NT])
        gate = sb("gate", [128, NT, 2])
        oneh = sb("oneh", [128, NT, E])
        comb = sb("comb", [128, NT, E])
        combT = sb("combT", [E, TOK])
        prob = each("prob", [128, 2, 512], scope=attention_memory)
        probT = each("probT", [128, 2, 512], scope=attention_memory)
        kM = each("kM", [128, HEADS, T], n=2, scope=attention_memory)
        rb = each("rb", [128, TT, HEADS, HP], n=2, scope=attention_memory)
        rT = each("rT", [128, 512], n=2, scope=attention_memory)
        attnT = each("attnT", [128, HG, 128], n=2, scope=attention_memory)
        attention_memory.close()
        hb = each("hb", [128, HC, 512], n=2)
        hhi = each("hhi", [128, HC, 512], F32R, n=2)
        hlo = each("hlo", [128, HC, 512], F32R, n=2)
        yc = each("yc", [128, 512], n=2)
        xhi = sb("xhi", [128, TOK], F32R)
        xlo = sb("xlo", [128, TOK], F32R)
        comb_b = each("comb_b", [128, TOK], n=2)
        b2s = sb("b2s", [128, E])
        b1s = each("b1s", [128, HC], n=2)
        w_raw = each("w_raw", [128, 2, HID], n=2)
        w_hi = each("w_hi", [128, 2, HID], F32R, n=2)
        w_lo = each("w_lo", [128, 2, HID], F32R, n=2)
        acc = sb("acc", [128, TOK])

        consts_in, consts2_in, bias_in, out_stored = sem("consts_in"), sem("consts2_in"), sem("bias_in"), sem("out_stored")
        x_in = sems("x_in")
        w_in = sems("w_in", 2)
        b1_in = sems("b1_in", 2)
        dve_step, pool_pre, act_pre, casts_ready = sem("dve_step"), sem("pool_pre"), sem("act_pre"), sem("casts_ready")
        w_sums_ready, w_means_ready, w_eff_ready = sem("w_sums_ready"), sem("w_means_ready"), sem("w_eff_ready")
        cs_ready, gs_ready, ve_ready, rstd_ready, hn_ready = (
            sem(n) for n in ("cs_ready", "gs_ready", "ve_ready", "rstd_ready", "hn_ready"))
        qk_full, v_full, qk_ready, v_ready, s0_full, max0_ready, exp0_done, p0_ready, pT0_full, pT0_ready, av0_full, \
            at0_ready, proj0_full, x1_ready = (sem(n) for n in (
                "qk_full", "v_full", "qk_ready", "v_ready", "s0_full", "max0_ready", "exp0_done", "p0_ready",
                "pT0_full", "pT0_ready", "av0_full", "at0_ready", "proj0_full", "x1_ready"))
        sq_full, spad_ready, conv_full, conv_ready, x2_ready, tok_full = (
            sem(n) for n in ("sq_full", "spad_ready", "conv_full", "conv_ready", "x2_ready", "tok_full"))
        ln_ve, ln_rstd, ln_h, lnT_full, lnT_ready = (
            sem(n) for n in ("ln_ve", "ln_rstd", "ln_h", "lnT_full", "lnT_ready"))
        aqkv_full, aqk_ready, kM_ready, kM2_ready, av_ready, av_full, rb_ready, rT_full, rT_ready, attn_ready, \
            wo_full, t_ready = (sem(n) for n in (
                "aqkv_full", "aqk_ready", "kM_ready", "kM2_ready", "av_ready", "av_full", "rb_ready", "rT_full",
                "rT_ready", "attn_ready", "wo_full", "t_ready"))
        s_full, max_ready, exp_done, pT_full, pT_ready = (
            sems(n) for n in ("s_full", "max_ready", "exp_done", "pT_full", "pT_ready"))
        ffn_full, lg_full, lg_ready, split_ready, x_split = (
            sem(n) for n in ("ffn_full", "lg_full", "lg_ready", "split_ready", "x_split"))
        gap_ready, exp_gap, comb_ready, combT_full, combT_ready, routes_stored = (
            sem(n) for n in ("gap_ready", "exp_gap", "comb_ready", "combT_full", "combT_ready", "routes_stored"))
        comb_in = sems("comb_in", 2)
        whi_ready, w_ready = sem("whi_ready"), sem("w_ready")
        h_full, h_ready, hlo_ready = sem("h_full"), sem("h_ready"), sem("hlo_ready")
        hhi_ready = [sem("hhi_even_ready"), sem("hhi_odd_ready")]
        y_full, yc_ready, acc_ready = sem("y_full"), sem("yc_ready"), sem("acc_ready")

        A_WQ, A_WK, A_WV, A_WO = ([const(f"{layer}{n}") for layer in "ac"] for n in "qkvo")
        A_MASK = [[masks_bf["band0"], masks_bf["band1"]], [masks_bf["causal0"], masks_bf["causal1"]]]

        def unit_query(u):
            return 0 if u < 2 else 1

        def unit_heads(u):
            return range(4 * u, 4 * u + 4) if u < 2 else range(2 * (u - 2), 2 * (u - 2) + 2)

        def tiles(ap):
            return ap.rearrange("q (i c) -> q i c", i=TT)

        block = ctx.enter_context(nc.Block())

        @block.sync
        def _(sp):
            for n in range(B):
                sp.dma_start(xs[n][:, :], x[n]).then_inc(x_in[n], 16)
            sp.dma_start(b2s[:, :], b2).then_inc(bias_in, 16)

            def load_weights(e, s):
                sp.dma_start(w_raw[s][:, 0, :], w1[bass.ds(e, 1)].rearrange("e c h -> c (e h)")).then_inc(w_in[s], 16)
                sp.dma_start(w_raw[s][:, 1, :].rearrange("p (j c) -> p j c", j=HC),
                             w2[bass.ds(e, 1)].rearrange("e (j p) c -> p (e j) c", p=128)).then_inc(w_in[s], 16)

            def load_biases(e, s):
                sp.dma_start(b1s[s][:, :], b1[bass.ds(e, 1)].rearrange("e p j -> p (e j)")).then_inc(b1_in[s], 16)

            def load_routes(e, s):
                sp.dma_start(comb_b[s][:, :], routes[bass.ds(e, 1)].to_broadcast([128, TOK])).then_inc(comb_in[s], 16)

            load_weights(0, 0)
            load_weights(1, 1)
            load_biases(0, 0)
            load_biases(1, 1)
            sp.wait_ge(combT_ready, 1)
            sp.dma_start(routes, combT[:, :]).then_inc(routes_stored, 16)
            sp.wait_ge(routes_stored, 16)
            load_routes(0, 0)
            load_routes(1, 1)
            with sp.Fori(1, E // 2) as it:
                for s in range(2):
                    sp.wait_ge(w_ready, it * 2 + (s - 1))
                    load_weights(it * 2 + s, s)
                    sp.wait_ge(yc_ready, it * 4 + (2 * s - 2))
                    load_routes(it * 2 + s, s)
                    load_biases(it * 2 + s, s)
            for h in range(2):
                sp.wait_ge(acc_ready, BLOCKS - 1 + h)
                for b in range(2 * h, 2 * h + 2):
                    sp.dma_start(out[b], acc[:, b * T:(b + 1) * T]).then_inc(out_stored, 16)
            sp.wait_ge(out_stored, 16 * B)

        @block.gpsimd
        def _(pool):
            G = nc.gpsimd
            G.memset(neghalf[:, :], -0.5).then_inc(pool_pre, 1)
            for n in range(B):
                G.memset(spad[n][:, :, :], 0.0).then_inc(pool_pre, 1)
                G.memset(vh[n][:, :, :, :], 0.0).then_inc(pool_pre, 1)
            pool.wait_ge(pool_pre, 1 + 2 * B)

            def power(value, n, ready, done, width):
                pool.wait_ge(ready, value)
                G.tensor_tensor(rstd[n][:, 0:width], ve[n][:, 0:width], neghalf[:, 0:width], ALU.pow).then_inc(done, 1)

            def masked_keys(a, n):
                pool.wait_ge(aqk_ready, a * B + n + 1)
                if n >= 2:
                    pool.wait_ge(s_full[n - 2], (a + 1) * UNITS)
                for h in range(HG, HEADS):
                    last = G.tensor_scalar(kM[n % 2][:, h, :], k[n][:, :], const("headmask", h, h + 1), 1.0,
                                           ALU.mult, ALU.mult)
                last.then_inc(kM2_ready, 1)

            for n in range(B):
                power(n + 1, n, ve_ready, rstd_ready, 1)
            for n in range(B):
                power(B + n + 1, n, ve_ready, rstd_ready, 1)
            for n in range(B):
                pool.wait_ge(conv_ready, n + 1)
                G.tensor_tensor(x1[n][:, :], x1[n][:, :], conv_out[n][:, :], ALU.add).then_inc(x2_ready, 1)
            for a in range(2):
                for n in range(B):
                    power(2 * a * B + n + 1, n, ln_ve, ln_rstd, TT)
                for n in range(B):
                    masked_keys(a, n)
                for n in range(B):
                    power((2 * a + 1) * B + n + 1, n, ln_ve, ln_rstd, TT)
            for n in range(B):
                cols = slice(n * T, (n + 1) * T)
                pool.wait_ge(lnT_ready, 3 * B + n + 1)
                G.tensor_copy(xhi[:, cols], hT[n][:, :]).then_inc(split_ready, 1)
                pool.wait_ge(split_ready, n + 1)
                G.tensor_tensor(xlo[:, cols], hT[n][:, :], xhi[:, cols].bitcast(F32), ALU.subtract).then_inc(x_split, 1)

            def split_weights(e2, s):
                G.tensor_copy(w_hi[s][:, :, :], w_raw[s][:, :, :]).then_inc(whi_ready, 1)
                pool.wait_ge(whi_ready, e2 + (s + 1))
                G.tensor_tensor(w_lo[s][:, :, :], w_raw[s][:, :, :], w_hi[s][:, :, :].bitcast(F32), ALU.subtract
                                ).then_inc(w_ready, 1)

            def add_up(e2, i):
                pool.wait_ge(yc_ready, e2 * 2 + (i + 1))
                cols = slice((i % 2) * 512, (i % 2 + 1) * 512)
                G.tensor_tensor(acc[:, cols], acc[:, cols], yc[i % 2][:, :], ALU.add).then_inc(acc_ready, 1)

            for s in range(2):
                pool.wait_ge(w_in[s], 32)
                split_weights(0, s)
            with pool.Fori(0, E // 2 - 1) as it:
                for i in range(4):
                    if i % 2 == 1:
                        pool.wait_ge(w_in[i // 2], it * 32 + 64)
                        pool.wait_ge(y_full, it * 4 + (i + 1))
                    add_up(it * 2, i)
                    if i % 2 == 1:
                        split_weights(it * 2 + 2, i // 2)
            for i in range(4):
                add_up(E - 2, i)

        @block.scalar
        def _(act):
            act.dma_start(pk[:, 0:EARLY], packed[:, 0:EARLY]).then_inc(consts_in, 16)
            act.dma_start(pk[:, EARLY:PACKED], packed[:, EARLY:PACKED]).then_inc(consts2_in, 16)
            act.wait_ge(consts_in, 16)
            nc.scalar.activation(bq_scaled[:, :], vec(BQ), ACT.Copy, scale=float(C) ** -0.5).then_inc(act_pre, 1)
            act.wait_ge(act_pre, 1)
            act.wait_ge(pool_pre, 1 + 2 * B)

            def copy(dst, src, scale=1.0):
                return nc.scalar.activation(dst, src, ACT.Copy, scale=scale)

            def turned(j, n):
                act.wait_ge(lnT_full, j * B + n + 1)
                copy(hT[n][:, :], two[n][0][:, 0:T]).then_inc(lnT_ready, 1)

            def queries_keys(a, n):
                act.wait_ge(aqkv_full, a * B + n + 1)
                copy(q[n][:, :], lane[n][0][:, 0:T], float(HD) ** -0.5)
                copy(k[n][:, :], lane[n][0][:, T:2 * T]).then_inc(aqk_ready, 1)

            def exps(a, n, u):
                act.wait_ge(max_ready[n], a * UNITS + u + 1)
                if u >= 2:
                    act.wait_ge(pT_full[n], a * UNITS + u - 1)
                width = 128 if u < 2 else 256
                for i, h in enumerate(unit_heads(u)):
                    last = nc.scalar.activation(
                        prob[n][:, u % 2, i * width:(i + 1) * width],
                        lane[n][u % 2][:, i * width:(i + 1) * width], ACT.Exp,
                        bias=negmax[n][:, unit_query(u), h:h + 1], accum_out=sums[n][:, unit_query(u), h:h + 1])
                last.then_inc(exp_done[n], 1)

            def probs_turned(a, n, u):
                act.wait_ge(pT_full[n], a * UNITS + u + 1)
                copy(probT[n][:, u % 2, :], lane[n][2][:, :]).then_inc(pT_ready[n], 1)

            def units(a, ns):
                for u in range(UNITS + 1):
                    for n in ns:
                        if u < UNITS:
                            exps(a, n, u)
                        if u >= 1 and (u - 1) % 2 == 1:
                            probs_turned(a, n, u - 1)

            def inverse_sums_turned(a, n):
                act.wait_ge(rT_full, a * B + n + 1)
                copy(rT[n % 2][:, :], lane[n][2][:, :]).then_inc(rT_ready, 1)

            def attention(a):
                queries_keys(a, 0)
                queries_keys(a, 1)
                units(a, (0, 1))
                queries_keys(a, 2)
                queries_keys(a, 3)
                inverse_sums_turned(a, 0)
                inverse_sums_turned(a, 1)
                units(a, (2, 3))
                inverse_sums_turned(a, 2)
                inverse_sums_turned(a, 3)

            for n in range(B):
                act.wait_ge(qk_full, n + 1)
                nc.scalar.activation(q[n][:, :], two[n][0][:, 0:T], ACT.Identity, bias=bq_scaled[:, :],
                                     scale=float(C) ** -0.5)
                nc.scalar.activation(k[n][:, :], two[n][0][:, T:2 * T], ACT.Identity, bias=vec(BK)
                                     ).then_inc(qk_ready, 1)
            for n in range(B):
                act.wait_ge(max0_ready, n + 1)
                for i in range(TT):
                    last = nc.scalar.activation(
                        prob[n][:, 0, i * T:(i + 1) * T], two[n][0][:, i * T:(i + 1) * T], ACT.Exp,
                        bias=negmax[n][:, 0, i:i + 1], accum_out=sums[n][:, 0, i:i + 1])
                last.then_inc(exp0_done, 1)
            for n in range(B):
                act.wait_ge(pT0_full, n + 1)
                copy(probT[n][:, 0, :], two[n][1][:, :]).then_inc(pT0_ready, 1)
            for n in range(B):
                act.wait_ge(av0_full, n + 1)
                nc.scalar.activation(at0[n][:, :], two[n][0][:, 0:T], ACT.Identity, bias=vec(BV)
                                     ).then_inc(at0_ready, 1)
            for n in range(B):
                act.wait_ge(sq_full, n + 1)
                for g in range(3):
                    last = nc.scalar.activation(
                        spad[n][32 * g:32 * g + 32, 1:HH + 1, 2 - g:2 - g + WW],
                        two[n][1][32 * g:32 * g + 32, 0:T].rearrange("c (y x) -> c y x", y=HH), ACT.Relu,
                        bias=vec(BSQ)[32 * g:32 * g + 32, :])
                last.then_inc(spad_ready, 1)
            for n in range(B):
                act.wait_ge(conv_full, n + 1)
                nc.scalar.activation(conv_out[n][:, :], two[n][0][:, 0:T], ACT.Relu, bias=vec(BCONV)
                                     ).then_inc(conv_ready, 1)
            for n in range(B):
                turned(0, n)
            attention(0)
            for n in range(B):
                turned(1, n)
            for n in range(B):
                turned(2, n)
            attention(1)
            for n in range(B):
                act.wait_ge(lnT_full, 3 * B + n + 1)
                copy(acc[:, n * T:(n + 1) * T], two[n][0][:, T:2 * T])
                copy(hT[n][:, :], two[n][0][:, 0:T]).then_inc(lnT_ready, 1)
            act.wait_ge(gap_ready, 1)
            nc.scalar.activation(gap[:, :], gap[:, :], ACT.Exp).then_inc(exp_gap, 1)

            def hidden(e2, i):
                s = i // 2
                if i % 2 == 0:
                    act.wait_ge(b1_in[s], e2 * 8 + 16)
                for j in range(HC):
                    act.wait_ge(h_full, e2 * (2 * HC) + (i * HC + j + 1))
                    nc.scalar.activation(hb[i % 2][:, j, :], bank[j][:, :], ACT.Relu, bias=b1s[s][:, j:j + 1]
                                         ).then_inc(h_ready, 1)
                    if j % 2 == 0:
                        nc.scalar.activation(hhi[i % 2][:, j, :], bank[j][:, :], ACT.Relu, bias=b1s[s][:, j:j + 1]
                                             ).then_inc(hhi_ready[0], 1)

            def turn_routes():
                act.wait_ge(combT_full, 1)
                for h in range(2):
                    last = copy(combT[:, h * 512:(h + 1) * 512], bank[6 + h][0:E, :])
                last.then_inc(combT_ready, 1)

            def expert_pair(e2, first=False):
                for i in range(4):
                    if i >= 2 or not first:
                        act.wait_ge(y_full, e2 * 2 + (i - 1))
                    hidden(e2, i)

            turn_routes()
            expert_pair(0, first=True)
            with act.Fori(1, E // 2) as it:
                expert_pair(it * 2)

        @block.tensor
        def _(pe):
            mm = nc.tensor.matmul

            def group_stats(j, n):
                pe.wait_ge(cs_ready, j * B + n + 1)
                mm(two[n][1][:, 0:2], const("group"), mv[n][:, 0, :], start=True, stop=True).then_inc(gs_ready, 1)

            def turn(j, n):
                pe.wait_ge(ln_h, j * B + n + 1)
                for i in range(TT):
                    last = nc.tensor.transpose(two[n][0][:, i * 128:(i + 1) * 128], ht[n][:, i, :], ident)
                last.then_inc(lnT_full, 1)

            def project(a, n):
                pe.wait_ge(lnT_ready, 2 * a * B + n + 1)
                if n >= 2:
                    pe.wait_ge(exp_done[n - 2], (a + 1) * UNITS)
                mm(lane[n][0][:, 0:T], A_WQ[a], hT[n][:, :], start=True, stop=True)
                mm(lane[n][0][:, T:2 * T], A_WK[a], hT[n][:, :], start=True, stop=True)
                for i in range(TT):
                    last = mm(lane[n][1][:, i * 128:(i + 1) * 128], hT[n][:, i * 128:(i + 1) * 128], A_WV[a],
                              start=True, stop=True)
                last.then_inc(aqkv_full, 1)

            def scores(a, n, u):
                if u == 0:
                    pe.wait_ge(kM_ready, a * B + n + 1)
                    pe.wait_ge(av_ready, a * B + n + 1)
                if u == 1:
                    pe.wait_ge(kM2_ready, a * B + n + 1)
                if u >= 2:
                    pe.wait_ge(exp_done[n], a * UNITS + u - 1)
                width = 128 if u < 2 else 256
                i, heads = unit_query(u), unit_heads(u)
                dst = lane[n][u % 2]
                mm(dst[:, :], ident_bf[:, :], A_MASK[a][i][:, :], start=True, stop=False, skip_group_check=True)
                mm(dst[:, :], q[n][:, i * 128:(i + 1) * 128], kM[n % 2][:, heads[0]:heads[-1] + 1, 0:width],
                   start=False, stop=True, skip_group_check=True).then_inc(s_full[n], 1)

            def turn_probs(a, n, u):
                pe.wait_ge(exp_done[n], a * UNITS + u + 1)
                if u == 0:
                    if n >= 2:
                        pe.wait_ge(t_ready, a * B + n - 1)
                    else:
                        pe.wait_ge(lnT_ready, 2 * a * B + n + 3)
                else:
                    pe.wait_ge(pT_ready[n], a * UNITS + u)
                for i in range(4):
                    last = nc.tensor.transpose(lane[n][2][:, i * 128:(i + 1) * 128],
                                               prob[n][:, u % 2, i * 128:(i + 1) * 128], ident)
                last.then_inc(pT_full[n], 1)

            def mix(a, n, u):
                pe.wait_ge(pT_ready[n], a * UNITS + u + 1)
                key_tiles = 1 if u < 2 else 2
                for kt in range(key_tiles):
                    for i, h in enumerate(unit_heads(u)):
                        g, r = divmod(h, HG)
                        col = (2 * g + unit_query(u)) * 128
                        at = (i * key_tiles + kt) * 128
                        last = mm(lane[n][3][HP * r:HP * r + HP, col:col + 128], vh[n][:, kt, h, :],
                                  probT[n][:, u % 2, at:at + 128],
                                  start=(kt == 0), stop=(kt == key_tiles - 1), tile_position=(0, HP * r))
                if u == UNITS - 1:
                    last.then_inc(av_full, 1)

            def turn_inverse_sums(a, n):
                pe.wait_ge(rb_ready, a * B + n + 1)
                for g in range(2):
                    for i in range(TT):
                        col = (2 * g + i) * 128
                        last = nc.tensor.transpose(
                            lane[n][2][:, col:col + 128],
                            rb[n % 2][:, i, HG * g:HG * g + HG, :].rearrange("q h d -> q (h d)"), ident)
                last.then_inc(rT_full, 1)

            def project_out(a, n):
                pe.wait_ge(attn_ready, a * B + n + 1)
                for i in range(TT):
                    for g in range(2):
                        last = mm(lane[n][2][:, i * 128:(i + 1) * 128], attnT[n % 2][:, 2 * g + i, :],
                                  A_WO[a][:, g * 128:(g + 1) * 128], start=(g == 0), stop=(g == 1))
                last.then_inc(wo_full, 1)

            def unit_step(a, ns, u):
                for n in ns:
                    if u < UNITS:
                        scores(a, n, u)
                    if 1 <= u <= UNITS:
                        turn_probs(a, n, u - 1)
                    if u >= 2:
                        mix(a, n, u - 2)

            def attention(a):
                project(a, 0)
                project(a, 1)
                for u in range(UNITS + 2):
                    unit_step(a, (0, 1), u)
                project(a, 2)
                project(a, 3)
                turn_inverse_sums(a, 0)
                turn_inverse_sums(a, 1)
                unit_step(a, (2, 3), 0)
                project_out(a, 0)
                project_out(a, 1)
                for u in range(1, UNITS + 2):
                    unit_step(a, (2, 3), u)
                for n in (2, 3):
                    turn_inverse_sums(a, n)
                for n in (2, 3):
                    project_out(a, n)

            pe.wait_ge(consts_in, 16)
            for n in range(B):
                group_stats(0, n)
            for n in range(B):
                pe.wait_ge(hn_ready, n + 1)
                mm(two[n][0][:, 0:T], const("wq"), hn[n][:, :], start=True, stop=True)
                mm(two[n][0][:, T:2 * T], const("wk"), hn[n][:, :], start=True, stop=True).then_inc(qk_full, 1)
                for i in range(TT):
                    last = mm(two[n][1][:, i * 128:(i + 1) * 128], hn[n][:, i * 128:(i + 1) * 128], const("wv"),
                              start=True, stop=True)
                last.then_inc(v_full, 1)
            for n in range(B):
                pe.wait_ge(qk_ready, n + 1)
                for i in range(TT):
                    last = mm(two[n][0][:, i * T:(i + 1) * T], q[n][:, i * 128:(i + 1) * 128], k[n][:, :],
                              start=True, stop=True)
                last.then_inc(s0_full, 1)
            for n in range(B):
                pe.wait_ge(p0_ready, n + 1)
                pe.wait_ge(v_ready, n + 1)
                for kt in range(TT):
                    for i in range(TT):
                        last = nc.tensor.transpose(
                            two[n][1][:, kt * T + i * 128:kt * T + (i + 1) * 128],
                            prob[n][:, 0, i * T + kt * 128:i * T + (kt + 1) * 128], ident)
                last.then_inc(pT0_full, 1)
            for n in range(B):
                pe.wait_ge(pT0_ready, n + 1)
                for kt in range(TT):
                    last = mm(two[n][0][:, 0:T], v0[n][:, kt * 128:(kt + 1) * 128],
                              probT[n][:, 0, kt * T:(kt + 1) * T], start=(kt == 0), stop=(kt == TT - 1))
                last.then_inc(av0_full, 1)
            for n in range(B):
                pe.wait_ge(at0_ready, n + 1)
                mm(two[n][0][:, 0:T], const("wp"), at0[n][:, :], start=True, stop=True).then_inc(proj0_full, 1)
            for n in range(B):
                group_stats(1, n)
            for n in range(B):
                pe.wait_ge(hn_ready, B + n + 1)
                mm(two[n][1][0:96, 0:T], const("squeeze"), hn[n][:, :], start=True, stop=True).then_inc(sq_full, 1)
            for n in range(B):
                pe.wait_ge(spad_ready, n + 1)
                for dy in range(3):
                    last = mm(two[n][0][:, 0:T], const("conv")[0:96, dy * 128:(dy + 1) * 128],
                              spad[n][:, dy:dy + HH, 1:1 + WW], start=(dy == 0), stop=(dy == 2))
                last.then_inc(conv_full, 1)
            for n in range(B):
                pe.wait_ge(x2_ready, n + 1)
                for i in range(TT):
                    last = nc.tensor.transpose(two[n][1][:, i * 128:(i + 1) * 128],
                                               x1[n][:, i * 128:(i + 1) * 128], ident)
                last.then_inc(tok_full, 1)
            pe.wait_ge(w_sums_ready, 1)
            mm(two[0][0][:, 0:2], const("mean"), w_sum[:, :], start=True, stop=True).then_inc(w_means_ready, 1)
            pe.wait_ge(casts_ready, 5)
            pe.wait_ge(w_eff_ready, 1)
            for n in range(B):
                turn(0, n)
            attention(0)
            for n in range(B):
                turn(1, n)
            for n in range(B):
                pe.wait_ge(lnT_ready, B + n + 1)
                for i in range(TT):
                    last = mm(two[n][1][:, i * 128:(i + 1) * 128], hT[n][:, i * 128:(i + 1) * 128], w_eff[:, :],
                              start=True, stop=True)
                last.then_inc(ffn_full, 1)
            for n in range(B):
                turn(2, n)
            attention(1)
            for n in range(B):
                pe.wait_ge(ln_h, 3 * B + n + 1)
                for i in range(TT):
                    nc.tensor.transpose(two[n][0][:, i * 128:(i + 1) * 128], ht[n][:, i, :], ident)
                    last = nc.tensor.transpose(two[n][0][:, T + i * 128:T + (i + 1) * 128], t[n][:, i, :], ident)
                last.then_inc(lnT_full, 1)
            for n in range(B):
                pe.wait_ge(lnT_ready, 3 * B + n + 1)
                for i in range(TT):
                    last = mm(two[n][1][:, i * E:(i + 1) * E], hT[n][:, i * 128:(i + 1) * 128], const("router"),
                              start=True, stop=True)
                last.then_inc(lg_full, 1)

            pe.wait_ge(lg_ready, B)
            pe.wait_ge(x_split, B)

            def hidden(e2, i, first=False):
                s, h = divmod(i, 2)
                cols = slice(h * 512, (h + 1) * 512)
                if h == 0:
                    pe.wait_ge(w_ready, e2 + (s + 1))
                for j in range(HC):
                    if not first:
                        pe.wait_ge(h_ready, e2 * (2 * HC) + (i * HC + j + 1 - HC))
                        if j % 2 == 0:
                            pe.wait_ge(hhi_ready[0], e2 * HC + (2 * i - 2 + j // 2 + 1))
                    chunk = slice(j * 128, (j + 1) * 128)
                    mm(bank[j][:, :], w_hi[s][:, 0, chunk], xhi[:, cols], start=True, stop=False)
                    mm(bank[j][:, :], w_hi[s][:, 0, chunk], xlo[:, cols], start=False, stop=False)
                    mm(bank[j][:, :], w_lo[s][:, 0, chunk], xhi[:, cols], start=False, stop=True).then_inc(h_full, 1)

            def down(e2, i, first):
                s, h = divmod(i, 2)
                if i >= 2 or not first:
                    pe.wait_ge(yc_ready, e2 * 2 + (i - 1))
                for j in range(HC):
                    chunk = slice(j * 128, (j + 1) * 128)
                    pe.wait_ge(hhi_ready[j % 2], e2 * HC + (2 * i + j // 2 + 1))
                    mm(bank[4 + i % 2][:, :], w_hi[s][:, 1, chunk], hhi[i % 2][:, j, :], start=(j == 0), stop=False)
                    mm(bank[4 + i % 2][:, :], w_lo[s][:, 1, chunk], hhi[i % 2][:, j, :], start=False, stop=False)
                    pe.wait_ge(hlo_ready, e2 * (2 * HC) + (i * HC + j + 1))
                    last = mm(bank[4 + i % 2][:, :], w_hi[s][:, 1, chunk], hlo[i % 2][:, j, :],
                              start=False, stop=(j == HC - 1))
                last.then_inc(y_full, 1)

            hidden(0, 0, first=True)
            pe.wait_ge(comb_ready, 1)
            for i in range(NT):
                last = nc.tensor.transpose(bank[6 + i // 4][0:E, (i % 4) * 128:(i % 4 + 1) * 128], comb[:, i, :], ident)
            last.then_inc(combT_full, 1)

            def expert_pair(e2, first=False, final=False):
                for i in range(4):
                    if i < 3:
                        hidden(e2, i + 1)
                    elif not final:
                        hidden(e2 + 2, 0)
                    down(e2, i, first)

            expert_pair(0, first=True)
            with pe.Fori(1, E // 2 - 1) as it:
                expert_pair(it * 2)
            expert_pair(E - 2, final=True)

        @block.vector
        def _(dve):
            V = nc.vector
            count = [0]

            def step(ins):
                count[0] += 1
                ins.then_inc(dve_step, 1)
                dve.wait_ge(dve_step, count[0])

            def channel_stats(j, n, src):
                step(V.bn_stats(stats[n][:, 0, :], src[n][:, :]))
                step(V.bn_aggr(mv[n][:, 0, :], stats[n][:, 0, :]))
                V.scalar_tensor_tensor(mv[n][:, 0, 1:2], mv[n][:, 0, 0:1], mv[n][:, 0, 0:1], mv[n][:, 0, 1:2],
                                       ALU.mult, ALU.add).then_inc(cs_ready, 1)

            def group_variance(j, n, eps):
                dve.wait_ge(gs_ready, j * B + n + 1)
                step(V.tensor_copy(gmv[n][:, :], two[n][1][:, 0:2]))
                step(V.tensor_tensor(gsq[n][:, :], gmv[n][:, 0:1], gmv[n][:, 0:1], ALU.mult))
                V.scalar_tensor_tensor(ve[n][:, 0:1], gmv[n][:, 1:2], eps, gsq[n][:, :], ALU.add, ALU.subtract
                                       ).then_inc(ve_ready, 1)

            def norm_variance(j, n):
                for i in range(TT):
                    last = V.bn_stats(stats[n][:, i, :], t[n][:, i, :])
                step(last)
                for i in range(TT):
                    last = V.bn_aggr(mv[n][:, i, :], stats[n][:, i, :])
                step(last)
                V.tensor_scalar(ve[n][:, :], mv[n][:, :, 1], 1e-5, None, ALU.add).then_inc(ln_ve, 1)

            def norm(j, n):
                dve.wait_ge(ln_rstd, j * B + n + 1)
                for i in range(TT):
                    last = V.tensor_scalar(ht[n][:, i, :], t[n][:, i, :], mv[n][:, i, 0:1], rstd[n][:, i:i + 1],
                                           ALU.subtract, ALU.mult)
                last.then_inc(ln_h, 1)

            def keys_values(a, n):
                dve.wait_ge(aqkv_full, a * B + n + 1)
                V.tensor_copy(vh[n][:, :, :, 0:HD],
                              lane[n][1][:, 0:T].rearrange("k (t h d) -> k t h d", t=TT, h=HEADS)).then_inc(av_ready, 1)
                dve.wait_ge(aqk_ready, a * B + n + 1)
                for h in range(HG):
                    last = V.tensor_scalar(kM[n % 2][:, h, :], k[n][:, :], const("headmask", h, h + 1), None, ALU.mult)
                last.then_inc(kM_ready, 1)

            def units(a, ns):
                for u in range(UNITS + 1):
                    for n in ns:
                        if u < UNITS:
                            dve.wait_ge(s_full[n], a * UNITS + u + 1)
                            heads = unit_heads(u)
                            V.tensor_reduce(negmax[n][:, unit_query(u), heads[0]:heads[-1] + 1],
                                            lane[n][u % 2][:, :].rearrange("q (h k) -> q h k", h=len(heads)),
                                            AX.X, ALU.max, negate=True).then_inc(max_ready[n], 1)
                        if u >= 1 and (u - 1) % 2 == 0:
                            dve.wait_ge(pT_full[n], a * UNITS + u)
                            V.tensor_copy(probT[n][:, (u - 1) % 2, :], lane[n][2][:, :]).then_inc(pT_ready[n], 1)

            def inverse_sums(a, n):
                dve.wait_ge(exp_done[n], (a + 1) * UNITS)
                if n >= 2:
                    dve.wait_ge(rT_full, a * B + n - 1)
                step(V.reciprocal(rinv[n][:, :, :], sums[n][:, :, :]))
                V.tensor_copy(rb[n % 2][:, :, :, :], rinv[n][:, :, :].unsqueeze(3).to_broadcast([128, TT, HEADS, HP])
                              ).then_inc(rb_ready, 1)

            def normalize(a, n):
                dve.wait_ge(rT_ready, a * B + n + 1)
                dve.wait_ge(av_full, a * B + n + 1)
                V.tensor_tensor(attnT[n % 2][:, :, :], lane[n][3][:, :].rearrange("d (n q) -> d n q", n=HG),
                                rT[n % 2][:, :].rearrange("d (n q) -> d n q", n=HG), ALU.mult).then_inc(attn_ready, 1)

            def add_attention(a, n):
                dve.wait_ge(wo_full, a * B + n + 1)
                V.tensor_tensor(t[n][:, :, :], tiles(lane[n][2][:, 0:T]), t[n][:, :, :], ALU.add).then_inc(t_ready, 1)
                dve.wait_ge(t_ready, a * B + n + 1)

            def attention(a):
                for n in (0, 1):
                    keys_values(a, n)
                units(a, (0, 1))
                for n in (0, 1):
                    inverse_sums(a, n)
                for n in (2, 3):
                    keys_values(a, n)
                for n in (0, 1):
                    normalize(a, n)
                for n in (0, 1):
                    add_attention(a, n)
                units(a, (2, 3))
                for n in (2, 3):
                    inverse_sums(a, n)
                for n in (2, 3):
                    normalize(a, n)
                for n in (2, 3):
                    add_attention(a, n)

            def binarized_output(n):
                dve.wait_ge(ffn_full, n + 1)
                step(V.tensor_tensor(fy[n][:, :, :], tiles(two[n][1][:, 0:T]), tiles(const("fb")), ALU.add))
                step(V.tensor_scalar(fz[n][:, :, :], fy[n][:, :, :], -1.0, 1.0, ALU.max, ALU.min))
                step(V.tensor_scalar(fz[n][:, :, :], fz[n][:, :, :], 7.0, ROUND, ALU.mult, ALU.add))
                step(V.tensor_scalar(fz[n][:, :, :], fz[n][:, :, :], ROUND, 1.0 / 7.0, ALU.subtract, ALU.mult))
                step(V.tensor_tensor(fz[n][:, :, :], fz[n][:, :, :], fy[n][:, :, :], ALU.subtract))
                step(V.tensor_tensor(fz[n][:, :, :], fz[n][:, :, :], fy[n][:, :, :], ALU.add))
                step(V.tensor_tensor(t[n][:, :, :], t[n][:, :, :], fz[n][:, :, :], ALU.add))

            for n in range(B):
                dve.wait_ge(x_in[n], 16)
                channel_stats(0, n, xs)
            for n in range(B):
                group_variance(0, n, 1e-6)
            dve.wait_ge(consts_in, 16)
            for n in range(B):
                dve.wait_ge(rstd_ready, n + 1)
                step(V.tensor_tensor(ga[n][:, :], rstd[n][:, 0:1], vec(GAMMA), ALU.mult))
                step(V.scalar_tensor_tensor(gb[n][:, :], gmv[n][:, 0:1], ga[n][:, 0:1], vec(BETA),
                                            ALU.mult, ALU.subtract))
                V.tensor_scalar(hn[n][:, :], xs[n][:, :], ga[n][:, 0:1], gb[n][:, 0:1],
                                ALU.mult, ALU.subtract).then_inc(hn_ready, 1)
            for n in range(B):
                dve.wait_ge(v_full, n + 1)
                V.tensor_copy(v0[n][:, :], two[n][1][:, 0:T]).then_inc(v_ready, 1)
            for n in range(B):
                dve.wait_ge(s0_full, n + 1)
                V.tensor_reduce(negmax[n][:, 0, 0:TT], two[n][0][:, :].rearrange("q (i k) -> q i k", i=TT),
                                AX.X, ALU.max, negate=True).then_inc(max0_ready, 1)
            for n in range(B):
                dve.wait_ge(exp0_done, n + 1)
                step(V.reciprocal(rinv[n][:, 0, 0:TT], sums[n][:, 0, 0:TT]))
                for i in range(TT):
                    last = V.tensor_scalar(prob[n][:, 0, i * T:(i + 1) * T], prob[n][:, 0, i * T:(i + 1) * T],
                                           rinv[n][:, 0, i:i + 1], None, ALU.mult)
                last.then_inc(p0_ready, 1)
            for n in range(B):
                dve.wait_ge(proj0_full, n + 1)
                V.scalar_tensor_tensor(x1[n][:, :], two[n][0][:, 0:T], vec(BP), xs[n][:, :], ALU.add, ALU.add
                                       ).then_inc(x1_ready, 1)
                dve.wait_ge(x1_ready, n + 1)
                channel_stats(1, n, x1)
            for n in range(B):
                group_variance(1, n, 1e-5)
            for n in range(B):
                dve.wait_ge(rstd_ready, B + n + 1)
                V.tensor_scalar(hn[n][:, :], x1[n][:, :], gmv[n][:, 0:1], rstd[n][:, 0:1],
                                ALU.subtract, ALU.mult).then_inc(hn_ready, 1)

            dve.wait_ge(consts2_in, 16)
            V.tensor_reduce(w_sum[:, 0:1], const("fw"), AX.X, ALU.add)
            V.tensor_reduce(w_sum[:, 1:2], const("fw"), AX.X, ALU.add, apply_absolute_value=True
                            ).then_inc(w_sums_ready, 1)
            V.tensor_copy(ident_bf[:, :], ident).then_inc(casts_ready, 1)
            for name, mask in masks_bf.items():
                V.tensor_copy(mask[:, :], const(name)).then_inc(casts_ready, 1)

            for n in range(B):
                dve.wait_ge(tok_full, n + 1)
                step(V.tensor_copy(t[n][:, :, :], tiles(two[n][1][:, 0:T])))
                norm_variance(0, n)
            dve.wait_ge(w_means_ready, 1)
            step(V.tensor_copy(w_mean[:, :], two[0][0][:, 0:2]))
            V.tensor_scalar(w_less[:, :], const("fw"), w_mean[:, 0:1], None, ALU.is_lt)
            step(V.tensor_scalar(w_eff[:, :], const("fw"), w_mean[:, 0:1], None, ALU.is_gt))
            step(V.tensor_tensor(w_eff[:, :], w_eff[:, :], w_less[:, :], ALU.subtract))
            step(V.tensor_tensor(w_eff[:, :], w_eff[:, :], const("fw"), ALU.subtract))
            step(V.tensor_tensor(w_eff[:, :], w_eff[:, :], const("fw"), ALU.add))
            V.tensor_scalar(w_eff[:, :], w_eff[:, :], w_mean[:, 1:2], None, ALU.mult).then_inc(w_eff_ready, 1)
            for n in range(B):
                norm(0, n)
            attention(0)
            for n in range(B):
                norm_variance(1, n)
            for n in range(B):
                norm(1, n)
            for n in range(B):
                binarized_output(n)
                norm_variance(2, n)
            for n in range(B):
                norm(2, n)
            attention(1)
            for n in range(B):
                norm_variance(3, n)
            for n in range(B):
                norm(3, n)
            for n in range(B):
                dve.wait_ge(lg_full, n + 1)
                V.tensor_copy(lg[:, n * TT:(n + 1) * TT, :],
                              two[n][1][:, 0:TT * E].rearrange("q (i e) -> q i e", i=TT)).then_inc(lg_ready, 1)

            dve.wait_ge(lg_ready, B)
            for i in range(NT):
                last = V.max(top[:, i, :], lg[:, i, :])
            step(last)
            V.tensor_tensor(gap[:, :], top[:, :, 1], top[:, :, 0], ALU.subtract).then_inc(gap_ready, 1)
            for i in range(NT):
                last = V.max_index(topi[:, i, :], top[:, i, :], lg[:, i, :])
            step(last)
            step(V.tensor_copy(topf[:, :, :], topi[:, :, 0:2]))
            dve.wait_ge(exp_gap, 1)
            step(V.tensor_scalar(den[:, :], gap[:, :], 1.0, None, ALU.add))
            step(V.reciprocal(gate[:, :, 0], den[:, :]))
            step(V.tensor_tensor(gate[:, :, 1], gap[:, :], gate[:, :, 0], ALU.mult))

            def wide(ap):
                return ap.unsqueeze(2).to_broadcast([128, NT, E])

            iota = const("iota").unsqueeze(1).to_broadcast([128, NT, E])
            V.tensor_tensor(comb[:, :, :], iota, wide(topf[:, :, 0]), ALU.is_equal)
            step(V.tensor_tensor(oneh[:, :, :], iota, wide(topf[:, :, 1]), ALU.is_equal))
            V.tensor_tensor(comb[:, :, :], comb[:, :, :], wide(gate[:, :, 0]), ALU.mult)
            step(V.tensor_tensor(oneh[:, :, :], oneh[:, :, :], wide(gate[:, :, 1]), ALU.mult))
            V.tensor_tensor(comb[:, :, :], comb[:, :, :], oneh[:, :, :], ALU.add).then_inc(comb_ready, 1)

            def split_hidden(e2, i, first=False):
                if i >= 2 or not first:
                    dve.wait_ge(y_full, e2 * 2 + (i - 1))
                for j in range(HC):
                    dve.wait_ge(h_ready, e2 * (2 * HC) + (i * HC + j + 1))
                    if j % 2 == 1:
                        V.tensor_copy(hhi[i % 2][:, j, :], hb[i % 2][:, j, :]).then_inc(hhi_ready[1], 1)
                    dve.wait_ge(hhi_ready[j % 2], e2 * HC + (2 * i + j // 2 + 1))
                    V.tensor_tensor(hlo[i % 2][:, j, :], hb[i % 2][:, j, :], hhi[i % 2][:, j, :].bitcast(F32),
                                    ALU.subtract).then_inc(hlo_ready, 1)

            def weigh(e2, i, first):
                s, h = divmod(i, 2)
                dve.wait_ge(y_full, e2 * 2 + i + 1)
                if h == 0:
                    dve.wait_ge(comb_in[s], e2 * 8 + 16)
                if i >= 2 or not first:
                    dve.wait_ge(acc_ready, e2 * 2 + (i - 1))
                V.scalar_tensor_tensor(yc[i % 2][:, :], bank[4 + i % 2][:, :], b2s[:, bass.ds(e2 + s, 1)],
                                       comb_b[s][:, h * 512:(h + 1) * 512], ALU.add, ALU.mult).then_inc(yc_ready, 1)

            def expert_pair(e2, first=False, final=False):
                for i in range(4):
                    if i < 3:
                        split_hidden(e2, i + 1, first)
                    elif not final:
                        split_hidden(e2 + 2, 0)
                    weigh(e2, i, first)

            dve.wait_ge(bias_in, 16)
            split_hidden(0, 0, first=True)
            expert_pair(0, first=True)
            with dve.Fori(1, E // 2 - 1) as it:
                expert_pair(it * 2)
            expert_pair(E - 2, final=True)


def kernel(**inputs):
    import numpy as np
    import concourse.bacc as bacc
    from concourse.bass_utils import run_bass_kernel_spmd

    a = {n: np.asarray(v) for n, v in inputs.items()}
    f32 = np.float32

    def padded_rows(w):
        r = np.zeros((2, HG, HP, 128), f32)
        r[:, :, 0:HD] = w.reshape(2, HG, HD, 128)
        return r.reshape(2, 128, 128).transpose(1, 0, 2).reshape(128, 256)

    vecs = np.zeros((128, 8), f32)
    for i, n in ((GAMMA, "norm_gamma"), (BETA, "norm_beta"), (BQ, "bq"), (BK, "bk"), (BV, "bv"), (BP, "bp")):
        vecs[:, i] = a["L0_conv_" + n]
    squeeze = np.zeros((128, 96), f32)
    conv = np.zeros((128, 3, 128), f32)
    for g in range(3):
        squeeze[:, 32 * g:32 * g + SQ] = a["L1_conv_squeeze_w"].T
        vecs[32 * g:32 * g + SQ, BSQ] = a["L1_conv_squeeze_b"]
        for dy in range(3):
            conv[32 * g:32 * g + SQ, dy, 64:128] = a["L1_conv_expand3x3_w"][:, :, dy, g].T
    conv[32:32 + SQ, 1, 0:64] = a["L1_conv_expand1x1_w"].T
    vecs[0:64, BCONV] = a["L1_conv_expand1x1_b"]
    vecs[64:128, BCONV] = a["L1_conv_expand3x3_b"]

    qi = np.arange(128)[:, None]
    ki = np.arange(256)[None, :]

    def mask(valid, times):
        return np.tile(np.where(valid, 0.0, NEG).astype(f32), (1, times))

    band = [(ki <= qi + 128 * i) & (ki > qi + 128 * i - 64) for i in range(2)]
    causal = [ki <= qi + 128 * i for i in range(2)]
    ch = np.arange(128)
    parts = dict(
        ident=np.eye(128, dtype=f32), group=(ch[:, None] // 4 == ch[None, :] // 4).astype(f32) * f32(0.25),
        wq=a["L0_conv_wq"].T, wk=a["L0_conv_wk"].T, wv=a["L0_conv_wv"].T, wp=a["L0_conv_wp"].T, vecs=vecs,
        squeeze=squeeze, conv=conv.reshape(128, 384),
        aq=a["L2_attn_Wq"].T, ak=a["L2_attn_Wk"].T, av=a["L2_attn_Wv"].T, ao=padded_rows(a["L2_attn_Wo"].T),
        band0=mask(band[0][:, 0:128], 4), band1=mask(band[1], 2),
        fw=a["L2_ffn_weight"], fb=np.tile(a["L2_ffn_bias"][None, :], (128, 2)), mean=np.full((128, 128), 1.0 / C / C, f32),
        cq=a["L3_attn_W_Q"].reshape(128, 128).T, ck=a["L3_attn_W_K"].reshape(128, 128).T,
        cv=a["L3_attn_W_V"].reshape(128, 128).T, co=padded_rows(a["L3_attn_W_O"].T),
        causal0=mask(causal[0][:, 0:128], 4), causal1=mask(causal[1], 2),
        headmask=(ch[:, None] // HD == np.arange(HEADS)[None, :]).astype(f32), router=a["L3_ffn_W_router"],
       
        iota=np.tile(np.arange(8, dtype=f32)[None, :], (128, 1)),
    )
    assert list(parts) == list(WIDTHS)
    packed = np.concatenate([np.ascontiguousarray(parts[n]) for n in parts], axis=1)
    arrays = {
        "x": np.ascontiguousarray(a["x"].reshape(B, C, T)), "packed": packed,
        "b1": np.ascontiguousarray(a["L3_ffn_b1"].reshape(E, HC, 128).transpose(0, 2, 1)),
        "b2": np.ascontiguousarray(a["L3_ffn_b2"].T),
        "w1": np.ascontiguousarray(a["L3_ffn_W1"]), "w2": np.ascontiguousarray(a["L3_ffn_W2"]),
    }
    nc = bacc.Bacc("TRN2", target_bir_lowering=False, num_devices=1)
    ins = [nc.dram_tensor(n, v.shape, F32, kind="ExternalInput").ap() for n, v in arrays.items()]
    out = nc.dram_tensor("out", (B, C, T), F32, kind="ExternalOutput").ap()
    routes = nc.dram_tensor("routes", (E, TOK), F32, kind="Internal").ap()
    build(nc, *ins, routes, out)
    r = run_bass_kernel_spmd(nc, [arrays], core_ids=[0])
    return r.results[0]["out"].reshape(B, C, HH, WW)
```

```python
from contextlib import ExitStack

import concourse.bass as bass
from concourse import mybir

ALU = mybir.AluOpType
ACT = mybir.ActivationFunctionType
AX = mybir.AxisListType
F32 = mybir.dt.float32
BF16 = mybir.dt.bfloat16
F32R = mybir.dt.float32r
U32 = mybir.dt.uint32

C = 128
B, HH, WW = 4, 16, 16
T = HH * WW
TT = T // 128
NT = B * TT
HEADS, HD = 8, 16
HP = 32
HG = 4
SQ = 16
PW = WW + 2
E, HID = 8, 512
HC = HID // 128
UNITS = 6
TOK = B * T
BLOCKS = 2 * E
NEG = -1e30
ROUND = 1.5 * 2.0 ** 23

WIDTHS = dict(
    group=128, vecs=8, wq=128, wk=128, wv=128, ident=128, wp=128, squeeze=96, conv=3 * 128,
    aq=256, ak=256, av=128, ao=256, band0=512, band1=512, fw=128, fb=256, mean=128,
    cq=256, ck=256, cv=128, co=256, causal0=512, causal1=512, headmask=8, router=8,
    iota=8,
)
AT = {}
_at = 0
for _name, _width in WIDTHS.items():
    AT[_name] = _at
    _at += _width
PACKED = _at
FIRST = AT["wq"]
EARLY = AT["aq"]
GAMMA, BETA, BQ, BK, BV, BP, BSQ, BCONV = range(8)


def build(nc, x, packed, b1, b2, w1, w2, routes, out):
    with ExitStack() as ctx:
        attention_memory = ExitStack()

        def sb(name, shape, dt=F32, scope=ctx):
            return scope.enter_context(nc.sbuf_tensor(name, shape, dt))

        def each(name, shape, dt=F32, n=B, scope=ctx):
            return [sb(f"{name}{i}", shape, dt, scope) for i in range(n)]

        def sem(name):
            return ctx.enter_context(nc.semaphore(name))

        def sems(name, n=B):
            return [sem(f"{name}{i}") for i in range(n)]

        bank = [ctx.enter_context(nc.psum_tensor(f"bank{i}", [128, 512], F32)) for i in range(8)]
        two = [bank[4 * (n % 2) + 2 * (n // 2):][:2] for n in range(B)]
        lane = [bank[4 * (n % 2):][:4] for n in range(B)]

        h_bank = [lane[0][0], lane[0][1], lane[1][0], lane[1][1]]
        y_bank = [lane[0][3], lane[1][3]]
        r_bank = [lane[0][2], lane[1][2]]

        pk = sb("pk", [128, PACKED])

        def const(name, lo=0, hi=None):
            return pk[:, AT[name] + lo:AT[name] + (WIDTHS[name] if hi is None else hi)]

        def vec(i):
            return pk[:, AT["vecs"] + i:AT["vecs"] + i + 1]

        ident = const("ident")
        ident_bf = sb("ident_bf", [128, 128], BF16)
        masks_bf = {n: sb(f"{n}_bf", [128, 512], BF16) for n in ("band0", "band1", "causal0", "causal1")}
        neghalf = sb("neghalf", [128, B])
        bq_scaled = sb("bq_scaled", [128, 1])
        w_sum = sb("w_sum", [128, 2])
        w_mean = sb("w_mean", [128, 2])
        w_less = sb("w_less", [128, 128])
        w_eff = sb("w_eff", [128, 128])

        cmv = sb("cmv", [128, B, 2])
        csq = sb("csq", [128, B])
        gmv = sb("gmv", [128, B, 2])
        gsq = sb("gsq", [128, B])
        gve = sb("gve", [128, B])
        grstd = sb("grstd", [128, B])
        ga = sb("ga", [128, B])
        gb = sb("gb", [128, B])
        xs = each("xs", [128, T])
        stats = each("stats", [128, TT, 6])
        mv = each("mv", [128, TT, 2])
        ve = each("ve", [128, TT])
        rstd = each("rstd", [128, TT])
        hn = each("hn", [128, T])
        v0 = each("v0", [128, T])
        negmax = each("negmax", [128, 2, HEADS])
        sums = each("sums", [128, 2, HEADS])
        rinv = each("rinv", [128, 2, HEADS])
        at0 = each("at0", [128, T])
        x1 = each("x1", [128, T])
        spad = each("spad", [96, HH + 2, PW])
        conv_out = each("conv_out", [128, T])
        t = each("t", [128, TT, 128])
        ht = each("ht", [128, TT, 128])
        hT = each("hT", [128, T])
        fy = each("fy", [128, TT, 128])
        fz = each("fz", [128, TT, 128])
        vh = each("vh", [128, TT, HEADS, HP])
        lg = sb("lg", [128, NT, E])
        top = sb("top", [128, NT, 8])
        topi = sb("topi", [128, NT, 8], U32)
        topf = sb("topf", [128, NT, 2])
        gap = sb("gap", [128, NT])
        den = sb("den", [128, NT])
        gate = sb("gate", [128, NT, 2])
        oneh = sb("oneh", [128, NT, E])
        comb = sb("comb", [128, NT, E])
        prob = each("prob", [128, 2, 512], scope=attention_memory)
        probT = each("probT", [128, 2, 512], scope=attention_memory)
        first_memory = ExitStack()
        q = each("q", [128, T], scope=first_memory)
        k = each("k", [128, T], scope=first_memory)
        first_memory.close()
        kM = each("kM", [128, HEADS, T], F32R, n=2, scope=attention_memory)
        rb = each("rb", [128, TT, HEADS, HP], n=2, scope=attention_memory)
        rT = each("rT", [128, 512], n=2, scope=attention_memory)
        attnT = each("attnT", [128, HG, 128], n=2, scope=attention_memory)
        q_hi = each("q_hi", [128, 2, T], F32R, n=2, scope=attention_memory)
        q_lo = each("q_lo", [128, 2, T], F32R, n=2, scope=attention_memory)
        k_parts = each("k_parts", [128, 2, T], F32R, n=2, scope=attention_memory)
        attention_memory.close()
        hb = each("hb", [128, HC, 512], n=2)
        hhi = each("hhi", [128, HC, 512], F32R, n=2)
        hlo = each("hlo", [128, HC, 512], F32R, n=2)
        yc = each("yc", [128, 512], n=2)
        comb_b = each("comb_b", [128, TOK], n=2)
        combT = sb("combT", [E, TOK])
        sb("rest_of_attention_memory", [128, 2 * TOK])
        xhi = sb("xhi", [128, TOK], F32R)
        xlo = sb("xlo", [128, TOK], F32R)
        b2s = sb("b2s", [128, E])
        b1s = each("b1s", [128, HC], n=2)
        w_raw = each("w_raw", [128, 2, HID], n=2)
        w_hi = each("w_hi", [128, 2, HID], F32R, n=2)
        w_lo = each("w_lo", [128, 2, HID], F32R, n=2)
        acc = sb("acc", [128, TOK])

        group_in = sem("group_in")
        consts_in, consts2_in, bias_in, out_stored = (
            sem(n) for n in ("consts_in", "consts2_in", "bias_in", "out_stored"))
        x_in = sems("x_in")
        w1_in, w2_in = sems("w1_in", 2), sems("w2_in", 2)
        b1_in = sems("b1_in", 2)
        dve_step, pool_pre, act_pre, casts_ready = sem("dve_step"), sem("pool_pre"), sem("act_pre"), sem("casts_ready")
        w_sums_ready, w_means_ready, w_eff_ready = sem("w_sums_ready"), sem("w_means_ready"), sem("w_eff_ready")
        w_mean_read = sem("w_mean_read")
        cs_ready, gs_ready, ve_ready, rstd_ready, hn_ready = (
            sem(n) for n in ("cs_ready", "gs_ready", "ve_ready", "rstd_ready", "hn_ready"))
        qk_full, v_full, qk_ready, v_ready, s0_full, max0_ready, exp0_done, p0_ready, pT0_full, pT0_ready, av0_full, \
            at0_ready, proj0_full, x1_ready = (sem(n) for n in (
                "qk_full", "v_full", "qk_ready", "v_ready", "s0_full", "max0_ready", "exp0_done", "p0_ready",
                "pT0_full", "pT0_ready", "av0_full", "at0_ready", "proj0_full", "x1_ready"))
        sq_full, spad_ready, spad2_ready, conv_full, conv_ready, x2_ready, tok_full = (
            sem(n) for n in ("sq_full", "spad_ready", "spad2_ready", "conv_full", "conv_ready", "x2_ready", "tok_full"))
        ln_ve, ln_rstd, ln_h, lnT_full, lnT_ready = (
            sem(n) for n in ("ln_ve", "ln_rstd", "ln_h", "lnT_full", "lnT_ready"))
        aqk_full, k_hi_ready, q_hi_ready, k_parts_ready, q_lo_ready, atv_full = (
            sem(n) for n in ("aqk_full", "k_hi_ready", "q_hi_ready", "k_parts_ready", "q_lo_ready", "atv_full"))
        kM_ready, kM_act_ready, kM2_ready, av_ready = (
            sem(n) for n in ("kM_ready", "kM_act_ready", "kM2_ready", "av_ready"))
        av_full, rb_ready, rT_full, rT_ready, attn_ready, wo_full, t_ready = (
            sem(n) for n in ("av_full", "rb_ready", "rT_full", "rT_ready", "attn_ready", "wo_full", "t_ready"))
        s_full, max_ready, exp_done, pT_full, pT_ready = (
            sems(n) for n in ("s_full", "max_ready", "exp_done", "pT_full", "pT_ready"))
        ffn_full, ffn_copied, quantized, ffn_step, x3_ready = (
            sem(n) for n in ("ffn_full", "ffn_copied", "quantized", "ffn_step", "x3_ready"))
        lg_full, lg_ready, xlo01_ready, xlo23_ready = (
            sem(n) for n in ("lg_full", "lg_ready", "xlo01_ready", "xlo23_ready"))
        gap_ready, exp_gap, comb_ready, combT_full, combT_ready, routes_stored = (
            sem(n) for n in ("gap_ready", "exp_gap", "comb_ready", "combT_full", "combT_ready", "routes_stored"))
        comb_in = sems("comb_in", 2)
        w1hi_ready, w1_ready, w2hi_ready, w2_ready = (
            sem(n) for n in ("w1hi_ready", "w1_ready", "w2hi_ready", "w2_ready"))
        h_full, h_ready, hlo_ready = sem("h_full"), sem("h_ready"), sem("hlo_ready")
        hhi_ready = [sem("hhi_even_ready"), sem("hhi_odd_ready")]
        y_full, yc_ready, acc_ready = sem("y_full"), sem("yc_ready"), sem("acc_ready")

        A_WQ, A_WK, A_WV, A_WO = ([const(f"{layer}{n}") for layer in "ac"] for n in "qkvo")
        A_MASK = [[masks_bf["band0"], masks_bf["band1"]], [masks_bf["causal0"], masks_bf["causal1"]]]

        PAIRS = ((0, 1), (2, 3))
        PHASES = [(a, ns) for a in range(2) for ns in PAIRS]
        NORMS = [(0, n) for n in range(B)] + [(j, n) for ns in PAIRS for j in (1, 2) for n in ns] + [
            (3, n) for n in range(B)]

        ASIDE = (None, 1, 1, 3)
        STATS_STEP, NORM_STEP, TURN_STEP, PRODUCT_STEP, NEXT_STEP = 1, 2, 3, 4, 4
        WEIGHTS_STEP = 3

        def normed(j, n):
            return NORMS.index((j, n)) + 1

        def norm_bank(j, n):
            return (two[n][0], lane[n][2], lane[n][0], lane[n][2])[j]

        def logits_at(n):
            if n in PAIRS[1]:
                return y_bank[1][:, (n - 2) * TT * E:(n - 1) * TT * E]
            return lane[n][2][:, 0:TT * E]

        def other(n):
            return (n + 2) % B

        SCORE_BANKS = ((1, range(0, 2)), (0, range(0, 4)), (1, range(2, 4)),
                       (0, range(4, 8)), (1, range(4, 6)), (1, range(6, 8)))
        SECOND_HALF = next(u for u, (_, heads) in enumerate(SCORE_BANKS) if heads[0] >= HG)

        def unit_query(u):
            return SCORE_BANKS[u][0]

        def unit_heads(u):
            return SCORE_BANKS[u][1]

        def unit_width(u):
            return (unit_query(u) + 1) * 128

        def tiles(ap):
            return ap.rearrange("q (i c) -> q i c", i=TT)

        block = ctx.enter_context(nc.Block())

        @block.sync
        def _(sp):
            for n in range(B - 1):
                sp.dma_start(xs[n][:, :], x[n]).then_inc(x_in[n], 16)
            sp.dma_start(pk[:, FIRST:EARLY], packed[:, FIRST:EARLY]).then_inc(consts_in, 16)
            sp.dma_start(pk[:, EARLY:PACKED], packed[:, EARLY:PACKED]).then_inc(consts2_in, 16)
            sp.dma_start(b2s[:, :], b2).then_inc(bias_in, 16)

            def load_weights(e, s):
                sp.dma_start(w_raw[s][:, 0, :], w1[bass.ds(e, 1)].rearrange("e c h -> c (e h)")).then_inc(w1_in[s], 16)
                sp.dma_start(w_raw[s][:, 1, :].rearrange("p (j c) -> p j c", j=HC),
                             w2[bass.ds(e, 1)].rearrange("e (j p) c -> p (e j) c", p=128)).then_inc(w2_in[s], 16)

            def load_biases(e, s):
                sp.dma_start(b1s[s][:, :], b1[bass.ds(e, 1)].rearrange("e p j -> p (e j)")).then_inc(b1_in[s], 16)

            def load_routes(e, s):
                sp.dma_start(comb_b[s][:, :], routes[bass.ds(e, 1)].to_broadcast([128, TOK])).then_inc(comb_in[s], 16)

            load_weights(0, 0)
            load_weights(1, 1)
            load_biases(0, 0)
            load_biases(1, 1)
            for s in range(2):
                sp.wait_ge(w1_ready, s + 1)
                sp.wait_ge(w2_ready, s + 1)
                load_weights(s + 2, s)
            sp.wait_ge(combT_ready, 1)
            sp.dma_start(routes, combT[:, :]).then_inc(routes_stored, 16)
            sp.wait_ge(routes_stored, 16)
            load_routes(0, 0)
            load_routes(1, 1)
            with sp.Fori(1, E // 2 - 1) as it:
                for s in range(2):
                    sp.wait_ge(yc_ready, it * 4 + (2 * s - 2))
                    load_routes(it * 2 + s, s)
                    load_biases(it * 2 + s, s)
                    sp.wait_ge(w1_ready, it * 2 + (s + 1))
                    sp.wait_ge(w2_ready, it * 2 + (s + 1))
                    load_weights(it * 2 + (s + 2), s)
            for s in range(2):
                sp.wait_ge(yc_ready, BLOCKS - 6 + 2 * s)
                load_routes(E - 2 + s, s)
                load_biases(E - 2 + s, s)
            for h in range(2):
                sp.wait_ge(acc_ready, BLOCKS - 1 + h)
                for b in range(2 * h, 2 * h + 2):
                    sp.dma_start(out[b], acc[:, b * T:(b + 1) * T]).then_inc(out_stored, 16)
            sp.wait_ge(out_stored, 16 * B)

        @block.gpsimd
        def _(pool):
            G = nc.gpsimd
            G.memset(neghalf[:, :], -0.5).then_inc(pool_pre, 1)
            for n in range(B):
                G.memset(spad[n][:, :, :], 0.0).then_inc(pool_pre, 1)
                G.memset(vh[n][:, :, :, :], 0.0).then_inc(pool_pre, 1)
            pool.wait_ge(pool_pre, 1 + 2 * B)

            def power(j, n):
                pool.wait_ge(ln_ve, normed(j, n))
                G.tensor_tensor(rstd[n][:, :], ve[n][:, :], neghalf[:, 0:TT], ALU.pow).then_inc(ln_rstd, 1)

            def add_quantized(n):
                pool.wait_ge(quantized, n + 1)
                G.tensor_tensor(fz[n][:, :, :], fz[n][:, :, :], fy[n][:, :, :], ALU.subtract).then_inc(ffn_step, 1)
                pool.wait_ge(ffn_step, 2 * n + 1)
                G.tensor_tensor(fz[n][:, :, :], fz[n][:, :, :], fy[n][:, :, :], ALU.add).then_inc(ffn_step, 1)
                pool.wait_ge(ffn_step, 2 * n + 2)
                G.tensor_tensor(t[n][:, :, :], t[n][:, :, :], fz[n][:, :, :], ALU.add).then_inc(x3_ready, 1)

            def lower_tokens(n):
                cols = slice(n * T, (n + 1) * T)
                pool.wait_ge(lnT_ready, normed(3, n))
                G.tensor_tensor(xlo[:, cols], hT[n][:, :], xhi[:, cols].bitcast(F32), ALU.subtract
                                ).then_inc(xlo01_ready, 1)

            def masked_keys(a, n):
                pool.wait_ge(k_parts_ready, a * B + n + 1)
                for h in range(HG, HEADS):
                    last = G.tensor_scalar(kM[n % 2][:, h, :], k_parts[n % 2][:, h // HG, :].bitcast(F32),
                                           const("headmask", h, h + 1), 1.0, ALU.mult, ALU.mult)
                last.then_inc(kM2_ready, 1)

            for j in range(2):
                for p, ns in enumerate(PAIRS):
                    pool.wait_ge(ve_ready, 2 * j + p + 1)
                    of = slice(ns[0], ns[-1] + 1)
                    G.tensor_tensor(grstd[:, of], gve[:, of], neghalf[:, of], ALU.pow).then_inc(rstd_ready, 1)

            def lower_weights(e2, s, layer):
                pool.wait_ge((w1hi_ready, w2hi_ready)[layer], e2 + (s + 1))
                G.tensor_tensor(w_lo[s][:, layer, :], w_raw[s][:, layer, :], w_hi[s][:, layer, :].bitcast(F32),
                                ALU.subtract).then_inc((w1_ready, w2_ready)[layer], 1)

            for n in range(B):
                power(0, n)
            for a, ns in PHASES:
                for n in ns:
                    masked_keys(a, n)
                if (a, ns) == PHASES[0]:
                    for s in range(2):
                        for layer in range(2):
                            lower_weights(0, s, layer)
                    continue
                before = [other(n) for n in ns]
                if (a, ns) == PHASES[-1]:
                    for n in before:
                        power(3, n)
                    for n in before:
                        lower_tokens(n)
                else:
                    for n in before:
                        power(1, n)
                    for n in before:
                        add_quantized(n)
                    for n in before:
                        power(2, n)
            for n in PAIRS[1]:
                power(3, n)

            def add_up(e2, i):
                pool.wait_ge(yc_ready, e2 * 2 + (i + 1))
                cols = slice((i % 2) * 512, (i % 2 + 1) * 512)
                G.tensor_tensor(acc[:, cols], acc[:, cols], yc[i % 2][:, :], ALU.add).then_inc(acc_ready, 1)

            with pool.Fori(0, E // 2 - 1) as it:
                for i in range(4):
                    if i % 2 == 0:
                        lower_weights(it * 2 + 2, i // 2, 0)
                    add_up(it * 2, i)
                    if i % 2 == 1:
                        lower_weights(it * 2 + 2, i // 2, 1)
            for i in range(4):
                add_up(E - 2, i)

        @block.scalar
        def _(act):
            act.dma_start(pk[:, 0:FIRST], packed[:, 0:FIRST]).then_inc(group_in, 16)
            act.dma_start(xs[B - 1][:, :], x[B - 1]).then_inc(x_in[B - 1], 16)
            act.wait_ge(group_in, 16)
            nc.scalar.activation(bq_scaled[:, :], vec(BQ), ACT.Copy, scale=float(C) ** -0.5).then_inc(act_pre, 1)
            act.wait_ge(act_pre, 1)
            act.wait_ge(pool_pre, 1 + 2 * B)

            def copy(dst, src, scale=1.0):
                return nc.scalar.activation(dst, src, ACT.Copy, scale=scale)

            def turned(j, n):
                act.wait_ge(lnT_full, normed(j, n))
                if j == 3:
                    copy(xhi[:, n * T:(n + 1) * T], norm_bank(j, n)[:, 0:T])
                if j == 3 and n not in PAIRS[1]:
                    copy(acc[:, n * T:(n + 1) * T], norm_bank(j, n)[:, T:2 * T])
                copy(hT[n][:, :], norm_bank(j, n)[:, 0:T]).then_inc(lnT_ready, 1)

            def queries_keys(a, n):
                act.wait_ge(aqk_full, 2 * (a * B + n) + 1)
                copy(k_parts[n % 2][:, :, :], lane[n][1][:, :].rearrange("r (g t) -> r g t", g=2)
                     ).then_inc(k_hi_ready, 1)
                act.wait_ge(aqk_full, 2 * (a * B + n) + 2)
                copy(q_hi[n % 2][:, :, :], lane[n][0][:, :].rearrange("r (g t) -> r g t", g=2), float(HD) ** -0.5
                     ).then_inc(q_hi_ready, 1)

            def masked_keys(a, n):
                act.wait_ge(k_parts_ready, a * B + n + 1)
                for h in range(HG):
                    last = copy(kM[n % 2][:, h, :], k_parts[n % 2][:, 0, :].bitcast(F32), const("headmask", h, h + 1))
                last.then_inc(kM_act_ready, 1)

            def exps(a, n, u):
                act.wait_ge(max_ready[n], a * UNITS + u + 1)
                if u >= 2:
                    act.wait_ge(pT_full[n], a * UNITS + u - 1)
                width = unit_width(u)
                for i, h in enumerate(unit_heads(u)):
                    last = nc.scalar.activation(
                        prob[n][:, u % 2, i * width:(i + 1) * width],
                        lane[n][u % 2][:, i * width:(i + 1) * width], ACT.Exp,
                        bias=negmax[n][:, unit_query(u), h:h + 1], accum_out=sums[n][:, unit_query(u), h:h + 1])
                last.then_inc(exp_done[n], 1)

            def probs_turned(a, n, u):
                act.wait_ge(pT_full[n], a * UNITS + u + 1)
                copy(probT[n][:, u % 2, :], lane[n][2][:, :]).then_inc(pT_ready[n], 1)

            def units(a, ns, aside):
                for u in range(UNITS + 1):
                    for n in ns:
                        if aside and (u, n) in ((TURN_STEP - 1, ns[1]), (TURN_STEP, ns[0])):
                            turned(aside, other(n ^ 1))
                        if u >= 1 and (u - 1) % 2 == 1:
                            probs_turned(a, n, u - 1)
                        if u < UNITS:
                            exps(a, n, u)

            def inverse_sums_turned(a, n):
                act.wait_ge(rT_full, a * B + n + 1)
                copy(rT[n % 2][:, :], lane[n][2][:, :]).then_inc(rT_ready, 1)

            def first_queries_keys(n):
                act.wait_ge(qk_full, n + 1)
                nc.scalar.activation(q[n][:, :], two[n][0][:, 0:T], ACT.Identity, bias=bq_scaled[:, :],
                                     scale=float(C) ** -0.5)
                nc.scalar.activation(k[n][:, :], two[n][0][:, T:2 * T], ACT.Identity, bias=vec(BK)
                                     ).then_inc(qk_ready, 1)

            def first_exps(n):
                act.wait_ge(max0_ready, n + 1)
                for i in range(TT):
                    last = nc.scalar.activation(
                        prob[n][:, 0, i * T:(i + 1) * T], two[n][0][:, i * T:(i + 1) * T], ACT.Exp,
                        bias=negmax[n][:, 0, i:i + 1], accum_out=sums[n][:, 0, i:i + 1])
                last.then_inc(exp0_done, 1)

            def first_probs_turned(n):
                act.wait_ge(pT0_full, n + 1)
                copy(probT[n][:, 0, :], two[n][1][:, :]).then_inc(pT0_ready, 1)

            def first_mixed(n):
                act.wait_ge(av0_full, n + 1)
                nc.scalar.activation(at0[n][:, :], two[n][0][:, 0:T], ACT.Identity, bias=vec(BV)
                                     ).then_inc(at0_ready, 1)

            first_queries_keys(0)
            first_queries_keys(1)
            first_queries_keys(2)
            first_exps(0)
            first_queries_keys(3)
            first_exps(1)
            first_exps(2)
            first_exps(3)
            first_probs_turned(0)
            first_probs_turned(1)
            first_mixed(0)
            first_probs_turned(2)
            first_mixed(1)
            first_probs_turned(3)
            first_mixed(2)
            first_mixed(3)

            def squeezed(n):
                act.wait_ge(sq_full, n + 1)
                for g in range(2):
                    last = nc.scalar.activation(
                        spad[n][32 * g:32 * g + 32, 1:HH + 1, 2 - g:2 - g + WW],
                        two[n][1][32 * g:32 * g + 32, 0:T].rearrange("c (y x) -> c y x", y=HH), ACT.Relu,
                        bias=vec(BSQ)[32 * g:32 * g + 32, :])
                last.then_inc(spad_ready, 1)

            def convolved(n):
                act.wait_ge(conv_full, n + 1)
                nc.scalar.activation(conv_out[n][:, :], two[n][0][:, 0:T], ACT.Relu, bias=vec(BCONV)
                                     ).then_inc(conv_ready, 1)

            squeezed(0)
            squeezed(1)
            convolved(0)
            squeezed(2)
            squeezed(3)
            convolved(1)
            convolved(2)
            convolved(3)
            for n in PAIRS[0]:
                turned(0, n)
            for p, (a, ns) in enumerate(PHASES):
                if p >= 2:
                    for n in ns:
                        turned(2, n)
                for n in ns:
                    queries_keys(a, n)
                masked_keys(a, ns[1])
                if p == 0:
                    for n in PAIRS[1]:
                        turned(0, n)
                if p:
                    for n in ns:
                        inverse_sums_turned(PHASES[p - 1][0], other(n))
                units(a, ns, ASIDE[p])
            for n in PAIRS[1]:
                inverse_sums_turned(1, n)

            def hidden(e2, i):
                s = i // 2
                if i % 2 == 0:
                    act.wait_ge(b1_in[s], e2 * 8 + 16)
                for j in range(HC):
                    act.wait_ge(h_full, e2 * (2 * HC) + (i * HC + j + 1))
                    nc.scalar.activation(hb[i % 2][:, j, :], h_bank[j][:, :], ACT.Relu, bias=b1s[s][:, j:j + 1]
                                         ).then_inc(h_ready, 1)
                    if j % 2 == 0:
                        nc.scalar.activation(hhi[i % 2][:, j, :], h_bank[j][:, :], ACT.Relu, bias=b1s[s][:, j:j + 1]
                                             ).then_inc(hhi_ready[0], 1)

            def turn_routes():
                act.wait_ge(combT_full, 1)
                for h in range(2):
                    last = copy(combT[:, h * 512:(h + 1) * 512], r_bank[h][0:E, :])
                last.then_inc(combT_ready, 1)

            def expert_pair(e2, first=False):
                for i in range(1 if first else 0, 4):
                    if i >= 2 or not first:
                        act.wait_ge(y_full, e2 * 2 + (i - 1))
                    hidden(e2, i)
                    if i == 1 and first:
                        turn_routes()

            hidden(0, 0)
            for n in PAIRS[1]:
                turned(3, n)
            for n in PAIRS[1]:
                copy(acc[:, n * T:(n + 1) * T], norm_bank(3, n)[:, T:2 * T])
            act.wait_ge(gap_ready, 1)
            nc.scalar.activation(gap[:, :], gap[:, :], ACT.Exp).then_inc(exp_gap, 1)
            expert_pair(0, first=True)
            with act.Fori(1, E // 2) as it:
                expert_pair(it * 2)

        @block.tensor
        def _(pe):
            mm = nc.tensor.matmul

            def group_stats(j, p):
                pe.wait_ge(cs_ready, 2 * j + p + 1)
                ns = PAIRS[p]
                mm(two[ns[0]][1][:, 0:4], const("group"), cmv[:, ns[0]:ns[-1] + 1, :],
                   start=True, stop=True).then_inc(gs_ready, 1)

            def turn(j, n):
                pe.wait_ge(ln_h, normed(j, n))
                for i in range(TT):
                    last = nc.tensor.transpose(norm_bank(j, n)[:, i * 128:(i + 1) * 128], ht[n][:, i, :], ident)
                    if j == 3:
                        last = nc.tensor.transpose(norm_bank(j, n)[:, T + i * 128:T + (i + 1) * 128], t[n][:, i, :],
                                                   ident)
                last.then_inc(lnT_full, 1)

            def product(j, n):
                pe.wait_ge(lnT_ready, normed(j, n))
                for i in range(TT):
                    if j == 1:
                        last = mm(lane[n][2][:, T + i * 128:T + (i + 1) * 128], hT[n][:, i * 128:(i + 1) * 128],
                                  w_eff[:, :], start=True, stop=True)
                    else:
                        last = mm(logits_at(n)[:, i * E:(i + 1) * E], hT[n][:, i * 128:(i + 1) * 128],
                                  const("router"), start=True, stop=True)
                last.then_inc(ffn_full if j == 1 else lg_full, 1)

            def project(a, n):
                pe.wait_ge(lnT_ready, normed(2 * a, n))
                for dst, w in ((lane[n][1], A_WK[a]), (lane[n][0], A_WQ[a])):
                    for g in range(2):
                        last = mm(dst[:, g * T:(g + 1) * T], w[:, g * 128:(g + 1) * 128], hT[n][:, :],
                                  start=True, stop=True)
                    last.then_inc(aqk_full, 1)

            def values(a, n):
                pe.wait_ge(k_parts_ready, a * B + n + 1)
                for i in range(TT):
                    last = mm(lane[n][1][:, i * 128:(i + 1) * 128], hT[n][:, i * 128:(i + 1) * 128], A_WV[a],
                              start=True, stop=True)
                last.then_inc(atv_full, 1)

            def scores(a, n, u):
                if u == 0:
                    pe.wait_ge(q_lo_ready, a * B + n + 1)
                    pe.wait_ge((kM_ready, kM_act_ready)[n % 2], (a * B + n) // 2 + 1)
                if u == SECOND_HALF:
                    pe.wait_ge(kM2_ready, a * B + n + 1)
                if u == 1:
                    pe.wait_ge(av_ready, a * B + n + 1)
                if u >= 2:
                    pe.wait_ge(exp_done[n], a * UNITS + u - 1)
                width = unit_width(u)
                i, heads = unit_query(u), unit_heads(u)
                dst = lane[n][u % 2]
                g = heads[0] // HG
                for part in (q_hi, q_lo):
                    mm(dst[:, :], part[n % 2][:, g, i * 128:(i + 1) * 128],
                       kM[n % 2][:, heads[0]:heads[-1] + 1, 0:width],
                       start=(part is q_hi), stop=False, skip_group_check=True)
                mask = A_MASK[a][i]
                if a == 1 and i == 1:
                    dst, mask = (ap[:, :].rearrange("q (h k) -> q h k", k=T)[:, :, 128:T] for ap in (dst, mask))
                else:
                    dst, mask = dst[:, :], mask[:, :]
                mm(dst, ident_bf[:, :], mask, start=False, stop=True, skip_group_check=True).then_inc(s_full[n], 1)

            def turn_probs(a, n, u, aside):
                pe.wait_ge(exp_done[n], a * UNITS + u + 1)
                if u > 0:
                    pe.wait_ge(pT_ready[n], a * UNITS + u)
                elif (a, n // 2) == (0, 0):
                    pe.wait_ge(lnT_ready, normed(0, other(n)))
                else:
                    pe.wait_ge(t_ready, a * B + n - 1)
                if aside and u + 1 == TURN_STEP:
                    pe.wait_ge(lnT_ready, normed(aside, other(n)))
                if aside and u + 1 == PRODUCT_STEP:
                    pe.wait_ge(ffn_copied if aside == 1 else lg_ready, other(n) + 1)
                for i in range(4):
                    last = nc.tensor.transpose(lane[n][2][:, i * 128:(i + 1) * 128],
                                               prob[n][:, u % 2, i * 128:(i + 1) * 128], ident)
                last.then_inc(pT_full[n], 1)

            def mix(a, n, u):
                pe.wait_ge(pT_ready[n], a * UNITS + u + 1)
                key_tiles = unit_width(u) // 128
                for kt in range(key_tiles):
                    for i, h in enumerate(unit_heads(u)):
                        g, r = divmod(h, HG)
                        col = (2 * g + unit_query(u)) * 128
                        at = (i * key_tiles + kt) * 128
                        last = mm(lane[n][3][HP * r:HP * r + HP, col:col + 128], vh[n][:, kt, h, :],
                                  probT[n][:, u % 2, at:at + 128],
                                  start=(kt == 0), stop=(kt == key_tiles - 1), tile_position=(0, HP * r))
                if u == UNITS - 1:
                    last.then_inc(av_full, 1)

            def turn_inverse_sums(a, n):
                pe.wait_ge(rb_ready, a * B + n + 1)
                for g in range(2):
                    for i in range(TT):
                        col = (2 * g + i) * 128
                        last = nc.tensor.transpose(
                            lane[n][2][:, col:col + 128],
                            rb[n % 2][:, i, HG * g:HG * g + HG, :].rearrange("q h d -> q (h d)"), ident)
                last.then_inc(rT_full, 1)

            def project_out(a, n):
                pe.wait_ge(attn_ready, a * B + n + 1)
                for i in range(TT):
                    for g in range(2):
                        last = mm(lane[n][2][:, i * 128:(i + 1) * 128], attnT[n % 2][:, 2 * g + i, :],
                                  A_WO[a][:, g * 128:(g + 1) * 128], start=(g == 0), stop=(g == 1))
                last.then_inc(wo_full, 1)

            def unit_step(a, ns, u, aside, before=None):
                if u == 1 and before is not None:
                    for n in ns:
                        scores(a, n, u)
                    for n in ns:
                        project_out(before, other(n))
                    for n in ns:
                        turn_probs(a, n, u - 1, aside)
                    return
                for n in ns:
                    if u < UNITS:
                        scores(a, n, u)
                    for job, at in ((turn, TURN_STEP), (product, PRODUCT_STEP)):
                        if aside and (u, n) in ((at - 1, ns[1]), (at, ns[0])):
                            pe.wait_ge(pT_ready[n ^ 1], a * UNITS + at - 1)
                            job(aside, other(n ^ 1))
                    if 1 <= u <= UNITS:
                        turn_probs(a, n, u - 1, aside)
                    if u >= 2:
                        mix(a, n, u - 2)

            pe.wait_ge(group_in, 16)
            group_stats(0, 0)
            group_stats(0, 1)
            pe.wait_ge(consts_in, 16)

            def first_project(n):
                pe.wait_ge(hn_ready, n + 1)
                mm(two[n][0][:, 0:T], const("wq"), hn[n][:, :], start=True, stop=True)
                mm(two[n][0][:, T:2 * T], const("wk"), hn[n][:, :], start=True, stop=True).then_inc(qk_full, 1)
                for i in range(TT):
                    last = mm(two[n][1][:, i * 128:(i + 1) * 128], hn[n][:, i * 128:(i + 1) * 128], const("wv"),
                              start=True, stop=True)
                last.then_inc(v_full, 1)

            def first_scores(n):
                pe.wait_ge(qk_ready, n + 1)
                for i in range(TT):
                    last = mm(two[n][0][:, i * T:(i + 1) * T], q[n][:, i * 128:(i + 1) * 128], k[n][:, :],
                              start=True, stop=True)
                last.then_inc(s0_full, 1)

            def first_turn(n):
                pe.wait_ge(p0_ready, n + 1)
                pe.wait_ge(v_ready, n + 1)
                for kt in range(TT):
                    for i in range(TT):
                        last = nc.tensor.transpose(
                            two[n][1][:, kt * T + i * 128:kt * T + (i + 1) * 128],
                            prob[n][:, 0, i * T + kt * 128:i * T + (kt + 1) * 128], ident)
                last.then_inc(pT0_full, 1)

            def first_mix(n):
                pe.wait_ge(pT0_ready, n + 1)
                for kt in range(TT):
                    last = mm(two[n][0][:, 0:T], v0[n][:, kt * 128:(kt + 1) * 128],
                              probT[n][:, 0, kt * T:(kt + 1) * T], start=(kt == 0), stop=(kt == TT - 1))
                last.then_inc(av0_full, 1)

            def first_project_out(n):
                pe.wait_ge(at0_ready, n + 1)
                mm(two[n][0][:, 0:T], const("wp"), at0[n][:, :], start=True, stop=True).then_inc(proj0_full, 1)

            first_project(0)
            first_project(1)
            first_scores(0)
            first_project(2)
            first_scores(1)
            first_project(3)
            first_scores(2)
            first_scores(3)
            first_turn(0)
            first_turn(1)
            first_mix(0)
            pe.wait_ge(w_sums_ready, 1)
            mm(two[0][1][:, 8:10], const("mean"), w_sum[:, :], start=True, stop=True).then_inc(w_means_ready, 1)
            first_turn(2)
            first_mix(1)
            first_turn(3)
            first_project_out(0)
            first_project_out(1)
            first_mix(2)
            first_mix(3)
            group_stats(1, 0)
            first_project_out(2)
            first_project_out(3)

            def turn_tokens(n):
                pe.wait_ge(x2_ready, n + 1)
                for i in range(TT):
                    last = nc.tensor.transpose(two[n][1][:, i * 128:(i + 1) * 128],
                                               x1[n][:, i * 128:(i + 1) * 128], ident)
                last.then_inc(tok_full, 1)

            def squeeze(n):
                pe.wait_ge(hn_ready, B + n + 1)
                mm(two[n][1][0:96, 0:T], const("squeeze"), hn[n][:, :], start=True, stop=True).then_inc(sq_full, 1)

            def convolve(n):
                pe.wait_ge(spad_ready, n + 1)
                pe.wait_ge(spad2_ready, n + 1)
                for dy in range(3):
                    last = mm(two[n][0][:, 0:T], const("conv")[0:96, dy * 128:(dy + 1) * 128],
                              spad[n][:, dy:dy + HH, 1:1 + WW], start=(dy == 0), stop=(dy == 2))
                last.then_inc(conv_full, 1)

            squeeze(0)
            squeeze(1)
            group_stats(1, 1)
            convolve(0)
            squeeze(2)
            squeeze(3)
            convolve(1)
            turn_tokens(0)
            convolve(2)
            turn_tokens(1)
            convolve(3)
            turn_tokens(2)
            turn(0, 0)
            turn_tokens(3)
            turn(0, 1)
            for n in PAIRS[0]:
                project(0, n)
            pe.wait_ge(casts_ready, 3)
            for p, (a, ns) in enumerate(PHASES):
                if p == 1:
                    pe.wait_ge(casts_ready, 5)
                    pe.wait_ge(w_eff_ready, 1)
                if p:
                    for n in ns:
                        turn_inverse_sums(PHASES[p - 1][0], other(n))
                for n in ns:
                    values(a, n)
                unit_step(a, ns, 0, ASIDE[p])
                if p == 0:
                    for n in PAIRS[1]:
                        turn(0, n)
                for u in range(1, UNITS + 1):
                    unit_step(a, ns, u, ASIDE[p], PHASES[p - 1][0] if p else None)
                if p < len(PHASES) - 1:
                    following = PHASES[p + 1]
                    if p >= 1:
                        for n in following[1]:
                            turn(2, n)
                    for n in following[1]:
                        project(following[0], n)
                unit_step(a, ns, UNITS + 1, ASIDE[p])
            for n in PAIRS[1]:
                turn_inverse_sums(1, n)

            def hidden(e2, i, first=False, chunks=range(HC)):
                s, h = divmod(i, 2)
                cols = slice(h * 512, (h + 1) * 512)
                if h == 0:
                    pe.wait_ge(w1_ready, e2 + (s + 1))
                for j in chunks:
                    if not first:
                        pe.wait_ge(h_ready, e2 * (2 * HC) + (i * HC + j + 1 - HC))
                        if j % 2 == 0:
                            pe.wait_ge(hhi_ready[0], e2 * HC + (2 * i - 2 + j // 2 + 1))
                    chunk = slice(j * 128, (j + 1) * 128)
                    mm(h_bank[j][:, :], w_hi[s][:, 0, chunk], xhi[:, cols], start=True, stop=False)
                    mm(h_bank[j][:, :], w_hi[s][:, 0, chunk], xlo[:, cols], start=False, stop=False)
                    mm(h_bank[j][:, :], w_lo[s][:, 0, chunk], xhi[:, cols], start=False, stop=True).then_inc(h_full, 1)

            def down(e2, i, first, chunks=range(HC)):
                s, h = divmod(i, 2)
                if i >= 2 or not first:
                    pe.wait_ge(yc_ready, e2 * 2 + (i - 1))
                if h == 0:
                    pe.wait_ge(w2_ready, e2 + (s + 1))
                for j in chunks:
                    chunk = slice(j * 128, (j + 1) * 128)
                    pe.wait_ge(hhi_ready[j % 2], e2 * HC + (2 * i + j // 2 + 1))
                    mm(y_bank[i % 2][:, :], w_hi[s][:, 1, chunk], hhi[i % 2][:, j, :], start=(j == 0), stop=False)
                    mm(y_bank[i % 2][:, :], w_lo[s][:, 1, chunk], hhi[i % 2][:, j, :], start=False, stop=False)
                    pe.wait_ge(hlo_ready, e2 * (2 * HC) + (i * HC + j + 1))
                    last = mm(y_bank[i % 2][:, :], w_hi[s][:, 1, chunk], hlo[i % 2][:, j, :],
                              start=False, stop=(j == HC - 1))
                if chunks[-1] == HC - 1:
                    last.then_inc(y_full, 1)

            pe.wait_ge(xlo01_ready, 2)
            hidden(0, 0, first=True, chunks=range(HC // 2))
            for n in PAIRS[1]:
                project_out(1, n)
            hidden(0, 0, first=True, chunks=range(HC // 2, HC))
            down(0, 0, first=True, chunks=range(HC // 2))
            for n in PAIRS[1]:
                turn(3, n)
            for n in PAIRS[1]:
                product(3, n)
            down(0, 0, first=True, chunks=range(HC // 2, HC))
            pe.wait_ge(xlo23_ready, 2)

            def turn_routes():
                pe.wait_ge(comb_ready, 1)
                for i in range(NT):
                    last = nc.tensor.transpose(r_bank[i // 4][0:E, (i % 4) * 128:(i % 4 + 1) * 128],
                                               comb[:, i, :], ident)
                last.then_inc(combT_full, 1)

            def expert_pair(e2, first=False, final=False):
                for i in range(4):
                    if i < 3:
                        hidden(e2, i + 1)
                    elif not final:
                        hidden(e2 + 2, 0)
                    if i == 0 and first:
                        turn_routes()
                        continue
                    down(e2, i, first)

            expert_pair(0, first=True)
            with pe.Fori(1, E // 2 - 1) as it:
                expert_pair(it * 2)
            expert_pair(E - 2, final=True)

        @block.vector
        def _(dve):
            V = nc.vector
            count = [0]
            done = {}

            def step(ins):
                count[0] += 1
                ins.then_inc(dve_step, 1)
                dve.wait_ge(dve_step, count[0])

            def mark(ins):
                count[0] += 1
                ins.then_inc(dve_step, 1)
                return count[0]

            def channel_stats(j, p, src):
                ns = PAIRS[p]
                of = slice(ns[0], ns[-1] + 1)
                for n in ns:
                    if j == 0:
                        dve.wait_ge(x_in[n], 16)
                    done[n] = mark(V.bn_stats(stats[n][:, 0, :], src[n][:, :]))
                for n in ns:
                    dve.wait_ge(dve_step, done[n])
                    done[n] = mark(V.bn_aggr(cmv[:, n, :], stats[n][:, 0, :]))
                dve.wait_ge(dve_step, done[ns[-1]])
                step(V.tensor_tensor(csq[:, of], cmv[:, of, 0], cmv[:, of, 0], ALU.mult))
                V.tensor_tensor(cmv[:, of, 1], cmv[:, of, 1], csq[:, of], ALU.add).then_inc(cs_ready, 1)

            def group_variance(j, p, eps):
                ns = PAIRS[p]
                of = slice(ns[0], ns[-1] + 1)
                dve.wait_ge(gs_ready, 2 * j + p + 1)
                step(V.tensor_copy(gmv[:, of, :], two[ns[0]][1][:, 0:4].rearrange("c (n s) -> c n s", n=2)))
                step(V.tensor_tensor(gsq[:, of], gmv[:, of, 0], gmv[:, of, 0], ALU.mult))
                V.scalar_tensor_tensor(gve[:, of], gmv[:, of, 1], eps, gsq[:, of], ALU.add, ALU.subtract
                                       ).then_inc(ve_ready, 1)

            def norm_variance(ns):
                done = {}
                for n in ns:
                    for i in range(TT):
                        last = V.bn_stats(stats[n][:, i, :], t[n][:, i, :])
                    done[n] = mark(last)
                for n in ns:
                    dve.wait_ge(dve_step, done[n])
                    for i in range(TT):
                        last = V.bn_aggr(mv[n][:, i, :], stats[n][:, i, :])
                    done[n] = mark(last)
                for n in ns:
                    dve.wait_ge(dve_step, done[n])
                    V.tensor_scalar(ve[n][:, :], mv[n][:, :, 1], 1e-5, None, ALU.add).then_inc(ln_ve, 1)

            def norm(j, n):
                dve.wait_ge(ln_rstd, normed(j, n))
                for i in range(TT):
                    last = V.tensor_scalar(ht[n][:, i, :], t[n][:, i, :], mv[n][:, i, 0:1], rstd[n][:, i:i + 1],
                                           ALU.subtract, ALU.mult)
                last.then_inc(ln_h, 1)

            def lower_keys(a, n):
                dve.wait_ge(k_hi_ready, a * B + n + 1)
                low = k_parts[n % 2][64:128, :, :]
                V.tensor_tensor(low, lane[n][1][64:128, :].rearrange("r (g t) -> r g t", g=2), low.bitcast(F32),
                                ALU.subtract).then_inc(k_parts_ready, 1)

            def lower_queries(a, n):
                dve.wait_ge(q_hi_ready, a * B + n + 1)
                V.scalar_tensor_tensor(q_lo[n % 2][:, :, :], lane[n][0][:, :].rearrange("r (g t) -> r g t", g=2),
                                       float(HD) ** -0.5, q_hi[n % 2][:, :, :].bitcast(F32), ALU.mult, ALU.subtract
                                       ).then_inc(q_lo_ready, 1)

            def masked_keys(a, n):
                dve.wait_ge(k_parts_ready, a * B + n + 1)
                for h in range(HG):
                    last = V.tensor_scalar(kM[n % 2][:, h, :], k_parts[n % 2][:, 0, :].bitcast(F32),
                                           const("headmask", h, h + 1), None, ALU.mult)
                last.then_inc(kM_ready, 1)

            def copy_values(a, n):
                dve.wait_ge(atv_full, a * B + n + 1)
                V.tensor_copy(vh[n][:, :, :, 0:HD],
                              lane[n][1][:, 0:T].rearrange("k (t h d) -> k t h d", t=TT, h=HEADS)).then_inc(av_ready, 1)

            def largest(a, n, u):
                dve.wait_ge(s_full[n], a * UNITS + u + 1)
                heads = unit_heads(u)
                V.tensor_reduce(negmax[n][:, unit_query(u), heads[0]:heads[-1] + 1],
                                lane[n][u % 2][:, :].rearrange("q (h k) -> q h k", h=len(heads)),
                                AX.X, ALU.max, negate=True).then_inc(max_ready[n], 1)

            def units(a, ns, aside, a_before):
                before = [other(n) for n in ns]
                for u in range(UNITS + 1):
                    if u == 1 and a_before is not None:
                        for n in ns:
                            largest(a, n, u)
                        for n in before:
                            add_attention(a_before, n)
                    for n in ns:
                        if u == PRODUCT_STEP and aside == 1:
                            dve.wait_ge(ffn_full, other(n) + 1)
                            V.tensor_tensor(fy[other(n)][:, :, :], tiles(lane[n][2][:, T:2 * T]), tiles(const("fb")),
                                            ALU.add).then_inc(ffn_copied, 1)
                            quantize(other(n))
                        if u == PRODUCT_STEP and aside == 3:
                            logits(other(n))
                        if 0 < u < UNITS and not (u == 1 and a_before is not None):
                            largest(a, n, u)
                        if u == NORM_STEP and aside:
                            norm(aside, other(n))
                        if u >= 1 and (u - 1) % 2 == 0:
                            dve.wait_ge(pT_full[n], a * UNITS + u)
                            V.tensor_copy(probT[n][:, (u - 1) % 2, :], lane[n][2][:, :]).then_inc(pT_ready[n], 1)
                    if u == WEIGHTS_STEP - 1 and (a, ns) == PHASES[0]:
                        binarized_weight()
                    s = u - WEIGHTS_STEP
                    if s in (0, 1) and (a, ns) == PHASES[0]:
                        dve.wait_ge(w1_in[s], 16)
                        V.tensor_copy(w_hi[s][:, 0, :], w_raw[s][:, 0, :]).then_inc(w1hi_ready, 1)
                        dve.wait_ge(w2_in[s], 16)
                        V.tensor_copy(w_hi[s][:, 1, :], w_raw[s][:, 1, :]).then_inc(w2hi_ready, 1)
                    if u == STATS_STEP and aside:
                        norm_variance(before)
                    if u >= NEXT_STEP and u - NEXT_STEP < 2 and aside == 1:
                        m = before[u - NEXT_STEP]
                        dve.wait_ge(x3_ready, m + 1)
                        norm_variance([m])
                    if u == NEXT_STEP + 1 and aside == 1:
                        norm(2, before[0])

            def inverse_sums(a, n):
                dve.wait_ge(exp_done[n], (a + 1) * UNITS)
                step(V.reciprocal(rinv[n][:, :, :], sums[n][:, :, :]))
                V.tensor_copy(rb[n % 2][:, :, :, :], rinv[n][:, :, :].unsqueeze(3).to_broadcast([128, TT, HEADS, HP])
                              ).then_inc(rb_ready, 1)

            def normalize(a, n):
                dve.wait_ge(rT_ready, a * B + n + 1)
                dve.wait_ge(av_full, a * B + n + 1)
                V.tensor_tensor(attnT[n % 2][:, :, :], lane[n][3][:, :].rearrange("d (n q) -> d n q", n=HG),
                                rT[n % 2][:, :].rearrange("d (n q) -> d n q", n=HG), ALU.mult).then_inc(attn_ready, 1)

            def add_attention(a, n):
                dve.wait_ge(wo_full, a * B + n + 1)
                V.tensor_tensor(t[n][:, :, :], tiles(lane[n][2][:, 0:T]), t[n][:, :, :], ALU.add).then_inc(t_ready, 1)
                dve.wait_ge(t_ready, a * B + n + 1)

            def quantize(n):
                dve.wait_ge(ffn_copied, n + 1)
                step(V.tensor_scalar(fz[n][:, :, :], fy[n][:, :, :], -1.0, 1.0, ALU.max, ALU.min))
                step(V.tensor_scalar(fz[n][:, :, :], fz[n][:, :, :], 7.0, ROUND, ALU.mult, ALU.add))
                V.tensor_scalar(fz[n][:, :, :], fz[n][:, :, :], ROUND, 1.0 / 7.0,
                                ALU.subtract, ALU.mult).then_inc(quantized, 1)

            def logits(n):
                dve.wait_ge(lg_full, n + 1 if n in PAIRS[0] else B)
                V.tensor_copy(lg[:, n * TT:(n + 1) * TT, :],
                              logits_at(n).rearrange("q (i e) -> q i e", i=TT)).then_inc(lg_ready, 1)

            def normed_input(p):
                dve.wait_ge(rstd_ready, p + 1)
                for n in PAIRS[p]:
                    done[n] = mark(V.tensor_tensor(ga[:, n:n + 1], grstd[:, n:n + 1], vec(GAMMA), ALU.mult))
                for n in PAIRS[p]:
                    dve.wait_ge(dve_step, done[n])
                    done[n] = mark(V.scalar_tensor_tensor(gb[:, n:n + 1], gmv[:, n, 0:1], ga[:, n:n + 1], vec(BETA),
                                                          ALU.mult, ALU.subtract))
                for n in PAIRS[p]:
                    dve.wait_ge(dve_step, done[n])
                    V.tensor_scalar(hn[n][:, :], xs[n][:, :], ga[:, n:n + 1], gb[:, n:n + 1],
                                    ALU.mult, ALU.subtract).then_inc(hn_ready, 1)

            channel_stats(0, 0, xs)
            dve.wait_ge(group_in, 16)
            group_variance(0, 0, 1e-6)
            channel_stats(0, 1, xs)
            normed_input(0)
            group_variance(0, 1, 1e-6)
            normed_input(1)

            def first_values(n):
                dve.wait_ge(v_full, n + 1)
                V.tensor_copy(v0[n][:, :], two[n][1][:, 0:T]).then_inc(v_ready, 1)

            def first_largest(n):
                dve.wait_ge(s0_full, n + 1)
                V.tensor_reduce(negmax[n][:, 0, 0:TT], two[n][0][:, :].rearrange("q (i k) -> q i k", i=TT),
                                AX.X, ALU.max, negate=True).then_inc(max0_ready, 1)

            def first_probs(n):
                dve.wait_ge(exp0_done, n + 1)
                step(V.reciprocal(rinv[n][:, 0, 0:TT], sums[n][:, 0, 0:TT]))
                for i in range(TT):
                    last = V.tensor_scalar(prob[n][:, 0, i * T:(i + 1) * T], prob[n][:, 0, i * T:(i + 1) * T],
                                           rinv[n][:, 0, i:i + 1], None, ALU.mult)
                last.then_inc(p0_ready, 1)

            first_values(0)
            first_values(1)
            first_largest(0)
            first_values(2)
            first_largest(1)
            first_probs(0)
            first_values(3)
            first_largest(2)
            first_probs(1)
            first_largest(3)
            dve.wait_ge(consts2_in, 16)
            V.tensor_reduce(w_sum[:, 0:1], const("fw"), AX.X, ALU.add)
            V.tensor_reduce(w_sum[:, 1:2], const("fw"), AX.X, ALU.add, apply_absolute_value=True
                            ).then_inc(w_sums_ready, 1)
            first_probs(2)
            first_probs(3)
            V.tensor_copy(ident_bf[:, :], ident).then_inc(casts_ready, 1)
            for name in ("band0", "band1"):
                V.tensor_copy(masks_bf[name][:, :], const(name)).then_inc(casts_ready, 1)
            dve.wait_ge(w_means_ready, 1)
            V.tensor_copy(w_mean[:, :], two[0][1][:, 8:10]).then_inc(w_mean_read, 1)

            def binarized_weight():
                dve.wait_ge(w_mean_read, 1)
                V.tensor_scalar(w_less[:, :], const("fw"), w_mean[:, 0:1], None, ALU.is_lt)
                step(V.tensor_scalar(w_eff[:, :], const("fw"), w_mean[:, 0:1], None, ALU.is_gt))
                step(V.tensor_tensor(w_eff[:, :], w_eff[:, :], w_less[:, :], ALU.subtract))
                step(V.tensor_tensor(w_eff[:, :], w_eff[:, :], const("fw"), ALU.subtract))
                step(V.tensor_tensor(w_eff[:, :], w_eff[:, :], const("fw"), ALU.add))
                V.tensor_scalar(w_eff[:, :], w_eff[:, :], w_mean[:, 1:2], None, ALU.mult).then_inc(w_eff_ready, 1)
                for name in ("causal0", "causal1"):
                    V.tensor_copy(masks_bf[name][:, :], const(name)).then_inc(casts_ready, 1)

            def first_residual(n):
                dve.wait_ge(proj0_full, n + 1)
                V.scalar_tensor_tensor(x1[n][:, :], two[n][0][:, 0:T], vec(BP), xs[n][:, :], ALU.add, ALU.add
                                       ).then_inc(x1_ready, 1)

            def normed_residual(p):
                dve.wait_ge(rstd_ready, 2 + p + 1)
                for n in PAIRS[p]:
                    V.tensor_scalar(hn[n][:, :], x1[n][:, :], gmv[:, n, 0:1], grstd[:, n:n + 1],
                                    ALU.subtract, ALU.mult).then_inc(hn_ready, 1)

            def squeezed(n):
                dve.wait_ge(sq_full, n + 1)
                dve.wait_ge(spad_ready, n + 1)
                V.tensor_scalar(spad[n][64:96, 1:HH + 1, 0:WW],
                                two[n][1][64:96, 0:T].rearrange("c (y x) -> c y x", y=HH), vec(BSQ)[64:96, :], 0.0,
                                ALU.add, ALU.max).then_inc(spad2_ready, 1)

            for n in PAIRS[0]:
                first_residual(n)
            dve.wait_ge(x1_ready, 2)
            channel_stats(1, 0, x1)
            group_variance(1, 0, 1e-5)
            for n in PAIRS[1]:
                first_residual(n)
            normed_residual(0)
            dve.wait_ge(x1_ready, B)
            channel_stats(1, 1, x1)
            for n in PAIRS[0]:
                squeezed(n)
            group_variance(1, 1, 1e-5)
            normed_residual(1)
            for n in PAIRS[1]:
                squeezed(n)

            def second_residual(n):
                dve.wait_ge(conv_ready, n + 1)
                V.tensor_tensor(x1[n][:, :], x1[n][:, :], conv_out[n][:, :], ALU.add).then_inc(x2_ready, 1)

            def tokens(ns):
                for n in ns:
                    dve.wait_ge(tok_full, n + 1)
                    done[n] = mark(V.tensor_copy(t[n][:, :, :], tiles(two[n][1][:, 0:T])))
                for n in ns:
                    dve.wait_ge(dve_step, done[n])

            second_residual(0)
            second_residual(1)
            for n in PAIRS[0]:
                tokens([n])
                norm_variance([n])
            second_residual(2)
            norm(0, 0)
            second_residual(3)
            norm(0, 1)
            tokens(PAIRS[1])
            norm_variance(PAIRS[1])
            for p, (a, ns) in enumerate(PHASES):
                if p >= 2:
                    norm(2, ns[1])
                if p:
                    for n in ns:
                        inverse_sums(PHASES[p - 1][0], other(n))
                lower_keys(a, ns[0])
                lower_queries(a, ns[0])
                lower_keys(a, ns[1])
                masked_keys(a, ns[0])
                lower_queries(a, ns[1])
                if p == 0:
                    for n in PAIRS[1]:
                        norm(0, n)
                for n in ns:
                    copy_values(a, n)
                    largest(a, n, 0)
                if p:
                    for n in ns:
                        normalize(PHASES[p - 1][0], other(n))
                units(a, ns, ASIDE[p], PHASES[p - 1][0] if p else None)
            def split_hidden(e2, i, first=False, chunks=range(HC)):
                if i >= 2 or not first:
                    dve.wait_ge(y_full, e2 * 2 + (i - 1))
                for j in chunks:
                    dve.wait_ge(h_ready, e2 * (2 * HC) + (i * HC + j + 1))
                    if j % 2 == 1:
                        V.tensor_copy(hhi[i % 2][:, j, :], hb[i % 2][:, j, :]).then_inc(hhi_ready[1], 1)
                    dve.wait_ge(hhi_ready[j % 2], e2 * HC + (2 * i + j // 2 + 1))
                    V.tensor_tensor(hlo[i % 2][:, j, :], hb[i % 2][:, j, :], hhi[i % 2][:, j, :].bitcast(F32),
                                    ALU.subtract).then_inc(hlo_ready, 1)

            for n in PAIRS[1]:
                inverse_sums(1, n)
            for n in PAIRS[1]:
                normalize(1, n)
            split_hidden(0, 0, first=True, chunks=range(1))
            for n in PAIRS[1]:
                add_attention(1, n)
            norm_variance(PAIRS[1])
            split_hidden(0, 0, first=True, chunks=range(1, HC // 2))
            for n in PAIRS[1]:
                norm(3, n)
            split_hidden(0, 0, first=True, chunks=range(HC // 2, HC))
            for n in PAIRS[1]:
                cols = slice(n * T, (n + 1) * T)
                dve.wait_ge(lnT_ready, normed(3, n))
                V.tensor_tensor(xlo[:, cols], hT[n][:, :], xhi[:, cols].bitcast(F32), ALU.subtract
                                ).then_inc(xlo23_ready, 1)
            for n in PAIRS[1]:
                logits(n)
            dve.wait_ge(lg_ready, B)
            for i in range(NT):
                last = V.max(top[:, i, :], lg[:, i, :])
            step(last)
            V.tensor_tensor(gap[:, :], top[:, :, 1], top[:, :, 0], ALU.subtract).then_inc(gap_ready, 1)
            for i in range(NT):
                last = V.max_index(topi[:, i, :], top[:, i, :], lg[:, i, :])
            step(last)
            step(V.tensor_copy(topf[:, :, :], topi[:, :, 0:2]))
            dve.wait_ge(exp_gap, 1)
            step(V.tensor_scalar(den[:, :], gap[:, :], 1.0, None, ALU.add))
            step(V.reciprocal(gate[:, :, 0], den[:, :]))
            step(V.tensor_tensor(gate[:, :, 1], gap[:, :], gate[:, :, 0], ALU.mult))

            def wide(ap):
                return ap.unsqueeze(2).to_broadcast([128, NT, E])

            iota = const("iota").unsqueeze(1).to_broadcast([128, NT, E])
            V.tensor_tensor(comb[:, :, :], iota, wide(topf[:, :, 0]), ALU.is_equal)
            step(V.tensor_tensor(oneh[:, :, :], iota, wide(topf[:, :, 1]), ALU.is_equal))
            V.tensor_tensor(comb[:, :, :], comb[:, :, :], wide(gate[:, :, 0]), ALU.mult)
            step(V.tensor_tensor(oneh[:, :, :], oneh[:, :, :], wide(gate[:, :, 1]), ALU.mult))
            V.tensor_tensor(comb[:, :, :], comb[:, :, :], oneh[:, :, :], ALU.add).then_inc(comb_ready, 1)

            def upper_weights(e2, s, layer):
                dve.wait_ge((w1_in, w2_in)[layer][s], e2 * 8 + 16)
                V.tensor_copy(w_hi[s][:, layer, :], w_raw[s][:, layer, :]).then_inc((w1hi_ready, w2hi_ready)[layer], 1)

            def weigh(e2, i, first):
                s, h = divmod(i, 2)
                dve.wait_ge(y_full, e2 * 2 + i + 1)
                if h == 0:
                    dve.wait_ge(comb_in[s], e2 * 8 + 16)
                if i >= 2 or not first:
                    dve.wait_ge(acc_ready, e2 * 2 + (i - 1))
                V.scalar_tensor_tensor(yc[i % 2][:, :], y_bank[i % 2][:, :], b2s[:, bass.ds(e2 + s, 1)],
                                       comb_b[s][:, h * 512:(h + 1) * 512], ALU.add, ALU.mult).then_inc(yc_ready, 1)

            def expert_pair(e2, first=False, final=False):
                for i in range(4):
                    s = i // 2
                    if i < 3:
                        split_hidden(e2, i + 1, first)
                    elif not final:
                        split_hidden(e2 + 2, 0)
                    if i % 2 == 0 and not final:
                        upper_weights(e2 + 2, s, 0)
                    if first and i == 0:
                        continue
                    if first and i == 1:
                        weigh(e2, 0, first)
                    weigh(e2, i, first)
                    if i % 2 == 1 and not final:
                        upper_weights(e2 + 2, s, 1)

            dve.wait_ge(bias_in, 16)
            expert_pair(0, first=True)
            with dve.Fori(1, E // 2 - 1) as it:
                expert_pair(it * 2)
            expert_pair(E - 2, final=True)


def kernel(**inputs):
    import numpy as np
    import concourse.bacc as bacc
    from concourse.bass_utils import run_bass_kernel_spmd

    a = {n: np.asarray(v) for n, v in inputs.items()}
    f32 = np.float32

    def padded_rows(w):
        r = np.zeros((2, HG, HP, 128), f32)
        r[:, :, 0:HD] = w.reshape(2, HG, HD, 128)
        return r.reshape(2, 128, 128).transpose(1, 0, 2).reshape(128, 256)

    def twice(w):
        return np.concatenate([w[:, 0:64], w[:, 0:64], w[:, 64:128], w[:, 64:128]], axis=1)

    vecs = np.zeros((128, 8), f32)
    for i, n in ((GAMMA, "norm_gamma"), (BETA, "norm_beta"), (BQ, "bq"), (BK, "bk"), (BV, "bv"), (BP, "bp")):
        vecs[:, i] = a["L0_conv_" + n]
    squeeze = np.zeros((128, 96), f32)
    conv = np.zeros((128, 3, 128), f32)
    for g in range(3):
        squeeze[:, 32 * g:32 * g + SQ] = a["L1_conv_squeeze_w"].T
        vecs[32 * g:32 * g + SQ, BSQ] = a["L1_conv_squeeze_b"]
        for dy in range(3):
            conv[32 * g:32 * g + SQ, dy, 64:128] = a["L1_conv_expand3x3_w"][:, :, dy, g].T
    conv[32:32 + SQ, 1, 0:64] = a["L1_conv_expand1x1_w"].T
    vecs[0:64, BCONV] = a["L1_conv_expand1x1_b"]
    vecs[64:128, BCONV] = a["L1_conv_expand3x3_b"]

    qi = np.arange(128)[:, None]
    ki = np.arange(256)[None, :]

    def mask(valid, times):
        return np.tile(np.where(valid, 0.0, NEG).astype(f32), (1, times))

    band = [(ki <= qi + 128 * i) & (ki > qi + 128 * i - 64) for i in range(2)]
    causal = [ki <= qi + 128 * i for i in range(2)]
    ch = np.arange(128)
    parts = dict(
        group=(ch[:, None] // 4 == ch[None, :] // 4).astype(f32) * f32(0.25), vecs=vecs,
        wq=a["L0_conv_wq"].T, wk=a["L0_conv_wk"].T, wv=a["L0_conv_wv"].T, 
        ident=np.eye(128, dtype=f32), wp=a["L0_conv_wp"].T,
        squeeze=squeeze, conv=conv.reshape(128, 384),
        aq=twice(a["L2_attn_Wq"].T), ak=twice(a["L2_attn_Wk"].T), av=a["L2_attn_Wv"].T,
        ao=padded_rows(a["L2_attn_Wo"].T),
        band0=mask(band[0][:, 0:128], 4), band1=mask(band[1], 2),
        fw=a["L2_ffn_weight"], fb=np.tile(a["L2_ffn_bias"][None, :], (128, 2)),
        mean=np.full((128, 128), 1.0 / C / C, f32),
        cq=twice(a["L3_attn_W_Q"].reshape(128, 128).T), ck=twice(a["L3_attn_W_K"].reshape(128, 128).T),
        cv=a["L3_attn_W_V"].reshape(128, 128).T, co=padded_rows(a["L3_attn_W_O"].T),
        causal0=mask(causal[0][:, 0:128], 4), causal1=mask(causal[1], 2),
        headmask=(ch[:, None] % 64 // HD == np.arange(HEADS)[None, :] % HG).astype(f32), router=a["L3_ffn_W_router"],
        iota=np.tile(np.arange(8, dtype=f32)[None, :], (128, 1)),
    )
    assert list(parts) == list(WIDTHS)
    packed = np.concatenate([np.ascontiguousarray(parts[n]) for n in parts], axis=1)
    arrays = {
        "x": np.ascontiguousarray(a["x"].reshape(B, C, T)), "packed": packed,
        "b1": np.ascontiguousarray(a["L3_ffn_b1"].reshape(E, HC, 128).transpose(0, 2, 1)),
        "b2": np.ascontiguousarray(a["L3_ffn_b2"].T),
        "w1": np.ascontiguousarray(a["L3_ffn_W1"]), "w2": np.ascontiguousarray(a["L3_ffn_W2"]),
    }
    nc = bacc.Bacc("TRN2", target_bir_lowering=False, num_devices=1)
    ins = [nc.dram_tensor(n, v.shape, F32, kind="ExternalInput").ap() for n, v in arrays.items()]
    out = nc.dram_tensor("out", (B, C, T), F32, kind="ExternalOutput").ap()
    routes = nc.dram_tensor("routes", (E, TOK), F32, kind="Internal").ap()
    build(nc, *ins, routes, out)
    r = run_bass_kernel_spmd(nc, [arrays], core_ids=[0])
    return r.results[0]["out"].reshape(B, C, HH, WW)
```
